# Optimizing a Trainium2 kernel written in Bass

```python
import numpy as np
import jax
import jax.numpy as jnp

def _softmax(x, axis=-1):
    return jax.nn.softmax(x, axis=axis)

def _gelu(x):
    return jax.nn.gelu(x, approximate=True)

def _silu(x):
    return jax.nn.silu(x)

def _sigmoid(x):
    return jax.nn.sigmoid(x)

def _layernorm(x, axis=-1, eps=1e-05):
    m = jnp.mean(x, axis=axis, keepdims=True)
    v = jnp.var(x, axis=axis, keepdims=True)
    return (x - m) / jnp.sqrt(v + eps)

def _scatter_add(tgt, idx, src, axis=0):
    return tgt.at[idx].add(src)

def _segment_sum(src, seg, n):
    return jax.ops.segment_sum(src, seg, n)
kernel_name = 'mk_gnn_preln_d4_gnn_r32_195448'

def setup_inputs(seed: int=0):
    np.random.seed(seed)
    _w = jnp.asarray

    def _rec_inputs():
        import jax
        import jax.numpy as jnp
        _gk = jax.random.key(seed)
        x = 1.875e-05 + 1 * jax.random.normal(jax.random.fold_in(_gk, 1), (3125, 96), jnp.float32)
        src = jax.random.randint(jax.random.fold_in(_gk, 2), (100000,), 0, 3125, jnp.int32)
        dst = jax.random.randint(jax.random.fold_in(_gk, 3), (100000,), 0, 3125, jnp.int32)
        _o = jnp.argsort(dst, stable=True)
        src = src[_o]
        dst = dst[_o]
        edge_attr_16 = 0.000254156 + 0.999948 * jax.random.normal(jax.random.fold_in(_gk, 12), (100000, 16), jnp.float32)
        return (x, src, dst, edge_attr_16)
    x, src, dst, edge_attr_16 = _rec_inputs()

    def _L0_gnn_setup():
        import jax, jax.numpy as jnp
        import numpy as np
        N_NODES = 3125
        N_EDGES = 25000
        D_FEAT = 96
        BN_EPS = 1e-05

        def _graph_conv(src, dst, x, bias, n_nodes):
            ones = jnp.ones((src.shape[0],), dtype=x.dtype)
            out_deg = jax.ops.segment_sum(ones, src, num_segments=n_nodes)
            in_deg = jax.ops.segment_sum(ones, dst, num_segments=n_nodes)
            out_norm = jax.lax.rsqrt(jnp.clip(out_deg, 1.0, None))
            in_norm = jax.lax.rsqrt(jnp.clip(in_deg, 1.0, None))
            xs = x * out_norm[:, None]
            msgs = xs[src]
            agg = jax.ops.segment_sum(msgs, dst, num_segments=n_nodes)
            return agg * in_norm[:, None] + bias[None, :]

        def _batch_norm(h, gamma, beta):
            mean = jnp.mean(h, axis=0)
            var = jnp.mean(jnp.square(h - mean[None, :]), axis=0)
            return (h - mean[None, :]) * jax.lax.rsqrt(var + BN_EPS) * gamma[None, :] + beta[None, :]
        key = jax.random.key(seed)
        k1, k2, k3 = jax.random.split(key, 3)
        feature = jax.random.normal(k1, (N_NODES, D_FEAT), dtype=jnp.float32)
        src = jax.random.randint(k2, (N_EDGES,), 0, N_NODES, dtype=jnp.int32)
        dst = jax.random.randint(k3, (N_EDGES,), 0, N_NODES, dtype=jnp.int32)
        bias1 = jnp.zeros((D_FEAT,), dtype=jnp.float32)
        bias2 = jnp.zeros((D_FEAT,), dtype=jnp.float32)
        gamma = jnp.ones((D_FEAT,), dtype=jnp.float32)
        beta = jnp.zeros((D_FEAT,), dtype=jnp.float32)
        return {'feature': feature, 'src': src, 'dst': dst, 'bias1': bias1, 'bias2': bias2, 'gamma': gamma, 'beta': beta}
    _L0_gnn_all = _L0_gnn_setup()
    _L0_gnn_in = {k: v for k, v in _L0_gnn_all.items() if k in ('bias1', 'bias2', 'gamma', 'beta')}
    del _L0_gnn_all

    def _L1_gnn_setup():
        import jax, jax.numpy as jnp
        import numpy as np
        N_NODES = 50000
        N_EDGES = 25000
        D_IN = 96
        D_HID = 96
        D_OUT = 96

        def _mean_agg(x, src, dst, n_nodes):
            msg = x[src]
            summed = jax.ops.segment_sum(msg, dst, num_segments=n_nodes)
            deg = jax.ops.segment_sum(jnp.ones((src.shape[0],), x.dtype), dst, num_segments=n_nodes)
            return summed / jnp.maximum(deg, 1.0)[:, None]

        def _sage_conv(x, src, dst, W_self, W_neigh, b):
            agg = _mean_agg(x, src, dst, x.shape[0])
            return x @ W_self + agg @ W_neigh + b
        key = jax.random.key(seed)
        ks = jax.random.split(key, 9)
        s = 0.05
        return {'x': jax.random.normal(ks[0], (N_NODES, D_IN), jnp.float32), 'src': jax.random.randint(ks[1], (N_EDGES,), 0, N_NODES), 'dst': jax.random.randint(ks[2], (N_EDGES,), 0, N_NODES), 'W_self1': jax.random.normal(ks[3], (D_IN, D_HID), jnp.float32) * s, 'W_neigh1': jax.random.normal(ks[4], (D_IN, D_HID), jnp.float32) * s, 'b1': jnp.zeros((D_HID,), jnp.float32), 'W_self2': jax.random.normal(ks[5], (D_HID, D_OUT), jnp.float32) * s, 'W_neigh2': jax.random.normal(ks[6], (D_HID, D_OUT), jnp.float32) * s, 'b2': jnp.zeros((D_OUT,), jnp.float32)}
    _L1_gnn_all = _L1_gnn_setup()
    _L1_gnn_in = {k: v for k, v in _L1_gnn_all.items() if k in ('W_self1', 'W_neigh1', 'b1', 'W_self2', 'W_neigh2', 'b2')}
    del _L1_gnn_all

    def _L2_gnn_setup():
        import jax, jax.numpy as jnp
        import numpy as np
        NEG_SLOPE_ATT = 0.2
        NEG_SLOPE_ACT = 0.01
        EPS_GN = 1e-05

        def _leaky(x, s):
            return jnp.where(x >= 0, x, s * x)

        def _gat_conv(x, src, dst, W, a_src, a_dst, b, n_nodes):
            h = x @ W.T
            alpha_s = h @ a_src
            alpha_d = h @ a_dst
            e = _leaky(alpha_s[src] + alpha_d[dst], NEG_SLOPE_ATT)
            m = jax.ops.segment_max(e, dst, num_segments=n_nodes)
            ex = jnp.exp(e - m[dst])
            z = jax.ops.segment_sum(ex, dst, num_segments=n_nodes)
            alpha = ex / z[dst]
            msg = h[src] * alpha[:, None]
            out = jax.ops.segment_sum(msg, dst, num_segments=n_nodes) + b
            return out

        def _graph_norm(x, weight, bias, mean_scale):
            mean = jnp.mean(x, axis=0)
            xc = x - mean_scale * mean
            var = jnp.mean(xc * xc, axis=0)
            return weight * xc * jax.lax.rsqrt(var + EPS_GN) + bias
        key = jax.random.key(seed)
        ks = jax.random.split(key, 12)
        N, E, C, ED = (50000, 25000, 96, 16)
        sc = 1.0 / np.sqrt(C)
        inp = {'x': jax.random.normal(ks[0], (N, C), jnp.float32), 'edge_index': jax.random.randint(ks[1], (2, E), 0, N, jnp.int32), 'edge_attr': jax.random.normal(ks[2], (E, ED), jnp.float32), 'W1': jax.random.normal(ks[3], (C, C), jnp.float32) * sc, 'att_src1': jax.random.normal(ks[4], (C,), jnp.float32) * sc, 'att_dst1': jax.random.normal(ks[5], (C,), jnp.float32) * sc, 'b1': jnp.zeros((C,), jnp.float32), 'W2': jax.random.normal(ks[6], (C, C), jnp.float32) * sc, 'att_src2': jax.random.normal(ks[7], (C,), jnp.float32) * sc, 'att_dst2': jax.random.normal(ks[8], (C,), jnp.float32) * sc, 'b2': jnp.zeros((C,), jnp.float32), 'gn_weight': jnp.ones((C,), jnp.float32), 'gn_bias': jnp.zeros((C,), jnp.float32), 'gn_mean_scale': jnp.ones((C,), jnp.float32)}
        return inp
    _L2_gnn_all = _L2_gnn_setup()
    _L2_gnn_in = {k: v for k, v in _L2_gnn_all.items() if k in ('W1', 'att_src1', 'att_dst1', 'b1', 'W2', 'att_src2', 'att_dst2', 'b2', 'gn_weight', 'gn_bias', 'gn_mean_scale')}
    del _L2_gnn_all

    def _L3_gnn_setup():
        import jax, jax.numpy as jnp
        import numpy as np
        N_NODES = 50000
        N_EDGES = 25000
        D_FEAT = 96
        key = jax.random.key(seed)
        kx, ke = jax.random.split(key)
        x = jax.random.normal(kx, (N_NODES, D_FEAT), dtype=jnp.float32)
        edge_index = jax.random.randint(ke, (2, N_EDGES), 0, N_NODES, dtype=jnp.int64)
        return {'x': x, 'edge_index': edge_index, 'num_nodes': N_NODES}
    _L3_gnn_all = _L3_gnn_setup()
    _L3_gnn_in = {k: v for k, v in _L3_gnn_all.items() if k in ()}
    del _L3_gnn_all
    return {'x': x, 'src': src, 'dst': dst, 'edge_attr_16': edge_attr_16, 'L0_gnn_bias1': _L0_gnn_in['bias1'], 'L0_gnn_bias2': _L0_gnn_in['bias2'], 'L0_gnn_gamma': _L0_gnn_in['gamma'], 'L0_gnn_beta': _L0_gnn_in['beta'], 'L1_gnn_W_self1': _L1_gnn_in['W_self1'], 'L1_gnn_W_neigh1': _L1_gnn_in['W_neigh1'], 'L1_gnn_b1': _L1_gnn_in['b1'], 'L1_gnn_W_self2': _L1_gnn_in['W_self2'], 'L1_gnn_W_neigh2': _L1_gnn_in['W_neigh2'], 'L1_gnn_b2': _L1_gnn_in['b2'], 'L2_gnn_W1': _L2_gnn_in['W1'], 'L2_gnn_att_src1': _L2_gnn_in['att_src1'], 'L2_gnn_att_dst1': _L2_gnn_in['att_dst1'], 'L2_gnn_b1': _L2_gnn_in['b1'], 'L2_gnn_W2': _L2_gnn_in['W2'], 'L2_gnn_att_src2': _L2_gnn_in['att_src2'], 'L2_gnn_att_dst2': _L2_gnn_in['att_dst2'], 'L2_gnn_b2': _L2_gnn_in['b2'], 'L2_gnn_gn_weight': _L2_gnn_in['gn_weight'], 'L2_gnn_gn_bias': _L2_gnn_in['gn_bias'], 'L2_gnn_gn_mean_scale': _L2_gnn_in['gn_mean_scale']}

def reference(x, src, dst, edge_attr_16, L0_gnn_bias1, L0_gnn_bias2, L0_gnn_gamma, L0_gnn_beta, L1_gnn_W_self1, L1_gnn_W_neigh1, L1_gnn_b1, L1_gnn_W_self2, L1_gnn_W_neigh2, L1_gnn_b2, L2_gnn_W1, L2_gnn_att_src1, L2_gnn_att_dst1, L2_gnn_b1, L2_gnn_W2, L2_gnn_att_src2, L2_gnn_att_dst2, L2_gnn_b2, L2_gnn_gn_weight, L2_gnn_gn_bias, L2_gnn_gn_mean_scale):
    import jax
    import jax.numpy as jnp

    def _L0_gnn_ref(feature, src, dst, bias1, bias2, gamma, beta):
        import jax, jax.numpy as jnp
        import numpy as np
        N_NODES = 3125
        N_EDGES = 25000
        D_FEAT = 96
        BN_EPS = 1e-05

        def _graph_conv(src, dst, x, bias, n_nodes):
            ones = jnp.ones((src.shape[0],), dtype=x.dtype)
            out_deg = jax.ops.segment_sum(ones, src, num_segments=n_nodes)
            in_deg = jax.ops.segment_sum(ones, dst, num_segments=n_nodes)
            out_norm = jax.lax.rsqrt(jnp.clip(out_deg, 1.0, None))
            in_norm = jax.lax.rsqrt(jnp.clip(in_deg, 1.0, None))
            xs = x * out_norm[:, None]
            msgs = xs[src]
            agg = jax.ops.segment_sum(msgs, dst, num_segments=n_nodes)
            return agg * in_norm[:, None] + bias[None, :]

        def _batch_norm(h, gamma, beta):
            mean = jnp.mean(h, axis=0)
            var = jnp.mean(jnp.square(h - mean[None, :]), axis=0)
            return (h - mean[None, :]) * jax.lax.rsqrt(var + BN_EPS) * gamma[None, :] + beta[None, :]
        h = _graph_conv(src, dst, feature, bias1, N_NODES)
        h = _batch_norm(h, gamma, beta)
        h = jax.nn.sigmoid(h)
        h = _graph_conv(src, dst, h, bias2, N_NODES)
        return h

    def _L1_gnn_ref(x, src, dst, W_self1, W_neigh1, b1, W_self2, W_neigh2, b2):
        import jax, jax.numpy as jnp
        import numpy as np
        N_NODES = 50000
        N_EDGES = 25000
        D_IN = 96
        D_HID = 96
        D_OUT = 96

        def _mean_agg(x, src, dst, n_nodes):
            msg = x[src]
            summed = jax.ops.segment_sum(msg, dst, num_segments=n_nodes)
            deg = jax.ops.segment_sum(jnp.ones((src.shape[0],), x.dtype), dst, num_segments=n_nodes)
            return summed / jnp.maximum(deg, 1.0)[:, None]

        def _sage_conv(x, src, dst, W_self, W_neigh, b):
            agg = _mean_agg(x, src, dst, x.shape[0])
            return x @ W_self + agg @ W_neigh + b
        h = _sage_conv(x, src, dst, W_self1, W_neigh1, b1)
        h = jax.nn.relu(h)
        h = _sage_conv(h, src, dst, W_self2, W_neigh2, b2)
        return h

    def _L2_gnn_ref(x, edge_index, edge_attr, W1, att_src1, att_dst1, b1, W2, att_src2, att_dst2, b2, gn_weight, gn_bias, gn_mean_scale):
        import jax, jax.numpy as jnp
        import numpy as np
        NEG_SLOPE_ATT = 0.2
        NEG_SLOPE_ACT = 0.01
        EPS_GN = 1e-05

        def _leaky(x, s):
            return jnp.where(x >= 0, x, s * x)

        def _gat_conv(x, src, dst, W, a_src, a_dst, b, n_nodes):
            h = x @ W.T
            alpha_s = h @ a_src
            alpha_d = h @ a_dst
            e = _leaky(alpha_s[src] + alpha_d[dst], NEG_SLOPE_ATT)
            m = jax.ops.segment_max(e, dst, num_segments=n_nodes)
            ex = jnp.exp(e - m[dst])
            z = jax.ops.segment_sum(ex, dst, num_segments=n_nodes)
            alpha = ex / z[dst]
            msg = h[src] * alpha[:, None]
            out = jax.ops.segment_sum(msg, dst, num_segments=n_nodes) + b
            return out

        def _graph_norm(x, weight, bias, mean_scale):
            mean = jnp.mean(x, axis=0)
            xc = x - mean_scale * mean
            var = jnp.mean(xc * xc, axis=0)
            return weight * xc * jax.lax.rsqrt(var + EPS_GN) + bias
        N = x.shape[0]
        loops = jnp.arange(N, dtype=edge_index.dtype)
        src = jnp.concatenate([edge_index[0], loops])
        dst = jnp.concatenate([edge_index[1], loops])
        residual = x
        h = _gat_conv(x, src, dst, W1, att_src1, att_dst1, b1, N)
        h = _leaky(_graph_norm(h, gn_weight, gn_bias, gn_mean_scale), NEG_SLOPE_ACT)
        h = _gat_conv(h, src, dst, W2, att_src2, att_dst2, b2, N)
        h = _graph_norm(h, gn_weight, gn_bias, gn_mean_scale)
        return _leaky(h + residual, NEG_SLOPE_ACT)

    def _L3_gnn_ref(x, edge_index, num_nodes):
        import jax, jax.numpy as jnp
        import numpy as np
        N_NODES = 50000
        N_EDGES = 25000
        D_FEAT = 96
        row, col = (edge_index[0], edge_index[1])
        deg = jnp.bincount(row, length=num_nodes).astype(x.dtype)
        deg_inv_sqrt = jnp.where(deg > 0, jax.lax.rsqrt(jnp.maximum(deg, 1.0)), 0.0)
        norm = deg_inv_sqrt[row] * deg_inv_sqrt[col]
        msg = x[col] * norm[:, None]
        out = jax.ops.segment_sum(msg, row, num_segments=num_nodes)
        return out
    edge_index = jnp.stack([src, dst])
    h = jnp.maximum(_layernorm(x, axis=-1), 0.0)
    x = x + _L0_gnn_ref(h, src, dst, L0_gnn_bias1, L0_gnn_bias2, L0_gnn_gamma, L0_gnn_beta)
    h = jnp.maximum(_layernorm(x, axis=-1), 0.0)
    x = x + _L1_gnn_ref(h, src, dst, L1_gnn_W_self1, L1_gnn_W_neigh1, L1_gnn_b1, L1_gnn_W_self2, L1_gnn_W_neigh2, L1_gnn_b2)
    h = jnp.maximum(_layernorm(x, axis=-1), 0.0)
    x = x + _L2_gnn_ref(h, edge_index, edge_attr_16, L2_gnn_W1, L2_gnn_att_src1, L2_gnn_att_dst1, L2_gnn_b1, L2_gnn_W2, L2_gnn_att_src2, L2_gnn_att_dst2, L2_gnn_b2, L2_gnn_gn_weight, L2_gnn_gn_bias, L2_gnn_gn_mean_scale)
    h = jnp.maximum(_layernorm(x, axis=-1), 0.0)
    x = x + _L3_gnn_ref(h, edge_index, 3125)
    return x

_drawn_inputs = setup_inputs


def setup_inputs(seed=0):
    import zlib

    import numpy as np

    out = dict(_drawn_inputs(seed))
    spreads = {'L0_gnn_bias1': (0.0, 0.8),
     'L0_gnn_bias2': (0.0, 0.1),
     'L0_gnn_gamma': (1.0, 0.6),
     'L0_gnn_beta': (0.0, 0.364),
     'L1_gnn_b1': (0.0, 0.1),
     'L1_gnn_b2': (0.0, 0.1),
     'L2_gnn_b1': (0.0, 0.1),
     'L2_gnn_b2': (0.0, 0.1),
     'L2_gnn_gn_weight': (1.0, 0.2),
     'L2_gnn_gn_bias': (0.0, 0.1),
     'L2_gnn_gn_mean_scale': (1.0, 0.2)}
    factors = {}
    for name, (base, spread) in spreads.items():
        noise = np.random.default_rng([zlib.crc32(name.encode()), seed]).standard_normal(out[name].shape)
        drawn = base * np.exp(spread * noise) if base else spread * noise
        out[name] = jnp.asarray(drawn.astype(out[name].dtype))
    for name, factor in factors.items():
        out[name] = (out[name] * factor).astype(out[name].dtype)
    return out
```

```python
from collections import namedtuple
from contextlib import ExitStack

import concourse.bass as bass
from concourse import mybir

F32, F16 = mybir.dt.float32, mybir.dt.float16
I32 = mybir.dt.int32
ALU = mybir.AluOpType
ACT = mybir.ActivationFunctionType
AX = mybir.AxisListType.X

P = 128
N = 3125
E = 100000
C = 96
NT = -(-N // P)
NP = NT * P
LAST = N - (NT - 1) * P
G = 5
NG = NT // G

EP, EF = 125, E // 125
SRC_BITS = 12
W = 16
NW = -(-N // W)
WT = 5
PAIR = 2 * WT
WE = WT * P
STEP = 25
NS = EF // STEP
CODES = NT * W
BASE = 1024
RING = 4
LOADS = 7
LW = NW // LOADS
LOADS_AT_ONCE = 7
STORE_BEHIND = 3
LN_EPS = 1e-5


class Chain:

    def __init__(self, eng, sem):
        self.eng, self.sem, self.n, self.reg, self.per = eng, sem, 0, None, 0

    def value(self):
        return self.n if self.reg is None else self.reg * self.per + self.n

    def __call__(self, ins):
        ins.then_inc(self.sem, 1)
        self.n += 1
        self.eng.wait_ge(self.sem, self.value())

    def lag(self, ins):
        ins.then_inc(self.sem, 1)
        self.n += 1
        self.eng.wait_ge(self.sem, self.value() - 1)

    def later(self, ins):
        ins.then_inc(self.sem, 1)
        self.n += 1

    def all(self):
        self.eng.wait_ge(self.sem, self.value())

    def loop(self, reg, per):
        self.reg, self.per, self.n0 = reg, per, self.n

    def end(self, trips):
        assert self.n - self.n0 == self.per, (self.n, self.n0, self.per)
        self.reg, self.n = None, self.n0 + trips * self.per


def semaphores(nc, k, phase, names):
    held = namedtuple(phase, names)(*[nc.alloc_semaphore(f"{phase}_{n}") for n in names.split()])
    k.held.extend(held)
    return held


def clear_semaphores(nc, k):
    nc.clear_and_free_semaphores(k.held)
    nc.all_engine_barrier()
    k.held = []


def flat(ap):
    return ap.rearrange("p a b -> p (a b)")


def locate_and_load(nc, k, d):
    with ExitStack() as c:
        def sb(name, shape, dt):
            return c.enter_context(nc.sbuf_tensor(name, shape, dt))

        def sem(name):
            return nc.alloc_semaphore(name)

        src = sb("src_i", [EP, EF], I32)
        dst = sb("dst_i", [EP, EF], I32)
        key = sb("key_i", [EP, EF], I32)
        sample = sb("sample", [EP, NS], F32)
        bound = sb("bound", [EP, NW], F32)
        below = sb("below", [EP, NS, NW], F16)
        start_f = sb("start_f", [1, NW], F32)
        count_ps = c.enter_context(nc.psum_tensor("count_ps", [1, NW], F32))
        edges_in, x_in, pads = sem("edges_in"), sem("x_in"), sem("pads")
        bounds_ready, key_ready, key_out = sem("bounds_ready"), sem("key_ready"), sem("key_out")
        below_ready, count_ready = sem("below_ready"), sem("count_ready")
        dve_chain, pool_chain = sem("dve_chain0"), sem("pool_chain0")
        block = c.enter_context(nc.Block())

        @block.sync
        def _(sp):
            sp.dma_start(dst[:, :], d.dst.rearrange("(p f) -> p f", p=EP)).then_inc(edges_in, 16)
            sp.dma_start(src[:, :], d.src.rearrange("(p f) -> p f", p=EP)).then_inc(edges_in, 16)
            sp.wait_ge(pads, 1)
            sp.dma_start(k.X[:, 0:NT - 1, :], d.x[0:(NT - 1) * P, :].rearrange("(t p) f -> p t f", p=P)).then_inc(x_in, 16)
            sp.dma_start(k.X[0:LAST, NT - 1, :], d.x[(NT - 1) * P:N, :]).then_inc(x_in, 16)
            sp.wait_ge(key_ready, 1)
            sp.dma_start(d.keys.rearrange("(p f) -> p f", p=EP), key[:, :]).then_inc(key_out, 16)
            sp.wait_ge(x_in, 32)
            sp.wait_ge(key_out, 16)

        @block.gpsimd
        def _(pool):
            pool.iota(bound[:, :], pattern=[[W, NW]], base=0, channel_multiplier=0,
                      allow_small_or_imprecise_dtypes=True).then_inc(bounds_ready, 1)
            chain = Chain(pool, pool_chain)
            chain(pool.memset(k.ident[:, :], 0.0))
            chain(pool.affine_select(out=k.ident[:, :], in_=k.ident[:, :], compare_op=ALU.not_equal, fill=1.0,
                                     base=0, pattern=[[-1, P]], channel_multiplier=1))
            chain(pool.tensor_copy(k.ident_h[:, :], k.ident[:, :]))

        @block.vector
        def _(dve):
            chain = Chain(dve, dve_chain)
            dve.memset(k.X[:, NT - 1, :], 0.0).then_inc(pads, 1)
            chain(dve.memset(k.ones_h[:, :], 1.0))
            chain(dve.memset(k.ones[:, :], 1.0))
            dve.wait_ge(edges_in, 32)
            nc.vector.scalar_tensor_tensor(out=key[:, :], in0=dst[:, :], scalar=float(1 << SRC_BITS), in1=src[:, :],
                                           op0=ALU.mult, op1=ALU.add).then_inc(key_ready, 1)
            chain(dve.tensor_copy(sample[:, :], dst[:, :].rearrange("p (s j) -> p s j", j=STEP)[:, :, 0]))
            dve.wait_ge(bounds_ready, 1)
            for s in range(NS):
                last = dve.tensor_scalar(below[:, s, :], bound[:, :], sample[:, s:s + 1], None, ALU.is_gt)
            last.then_inc(below_ready, 1)
            dve.wait_ge(count_ready, 1)
            chain(dve.tensor_scalar(start_f[:, :], count_ps[:, :], -1.0, 0.0, ALU.add, ALU.max))
            chain(dve.tensor_scalar(k.start_i[:, :], start_f[:, :], float(STEP), float(E - WE), ALU.mult, ALU.min))

        @block.tensor
        def _(pe):
            pe.wait_ge(below_ready, 1)
            for s in range(NS):
                last = nc.tensor.matmul(count_ps[:, :], k.ones_h[0:EP, 0:1], below[:, s, :], start=s == 0, stop=s == NS - 1)
            last.then_inc(count_ready, 1)


def build_adjacency(nc, k, d):
    with ExitStack() as c:
        def sb(name, shape, dt):
            return c.enter_context(nc.sbuf_tensor(name, shape, dt))

        def sem(name):
            return nc.alloc_semaphore(name)

        ncol = NW * WT
        lcol = LW * WT
        window_keys = sb("window_keys", [P, ncol], I32)
        low_i = sb("low_i", [P, 3, lcol], I32)
        row = sb("row", [P, ncol], F16)
        code = window_keys[:, :].bitcast(F32)
        negative = sb("negative", [P, NW], F32)
        inside = sb("inside", [P, ncol], F16)
        own = sb("own", [P, ncol], F16)
        rows_iota = sb("rows_iota", [P, P, PAIR], F16)
        codes_iota = sb("codes_iota", [P, CODES], F16)
        hot_row = sb("hot_row", [P, RING // 2, P, PAIR], F16)
        hot_code = sb("hot_code", [P, RING, WT, CODES], F16)
        distance = sb("distance", [P, RING, CODES], F16)
        zeros = sb("zeros", [P, P], F16)
        inside_sum = sb("inside_sum", [P, 1], F32)
        missed = sb("missed", [1, 1], I32)
        this_window = sb("this_window", [P, 1], F32)
        counts = c.enter_context(nc.psum_tensor("counts", [P, RING, 512], F32))
        degree_ps = c.enter_context(nc.psum_tensor("degree_ps", [P, 512], F32))
        total_ps = c.enter_context(nc.psum_tensor("total_ps", [P, 512], F32))
        window_in = [sem(f"window_in{n}") for n in range(LOADS)]
        iotas = sem("iotas")
        hot_ready, counted, stored = sem("hot_ready"), sem("counted"), sem("stored")
        codes_ready, distance_ready, act_hot_ready = sem("codes_ready"), sem("distance_ready"), sem("act_hot_ready")
        degree_ready, total_ready, flag_ready = sem("degree_ready"), sem("total_ready"), sem("flag_ready")
        g_keys_in, g_hot_ready, g_counted, g_window_done, g_stored, g_degree_ready = (
            sem("g_keys_in"), sem("g_hot_ready"), sem("g_counted"), sem("g_window_done"), sem("g_stored"), sem("g_degree_ready"))
        zeros_ready, sum_ready = sem("zeros_ready"), sem("sum_ready")
        dve_chain, pool_chain = sem("dve_chain1"), sem("pool_chain1")
        block = c.enter_context(nc.Block())
        rounds = NW // RING
        batches = EF // WT
        g_code, g_place, g_window = code[0:EP, 0:EF], inside[0:EP, 0:EF], own[0:EP, 0:EF]

        def load_windows(eng, load, first, rounds):
            with eng.Fori(0, rounds) as r:
                at = [eng.value_load(k.start_i[0:1, bass.ds(r * LOADS_AT_ONCE + (load * LW + first + b), 1)], min_val=0, max_val=E - WE)
                      for b in range(LOADS_AT_ONCE)]
                for b in range(LOADS_AT_ONCE):
                    w = r * LOADS_AT_ONCE + (load * LW + first + b)
                    eng.dma_start(window_keys[:, bass.ds(w * WT, WT)],
                                  d.keys[bass.ds(at[b], WE)].rearrange("(p j) -> p j", j=WT)).then_inc(window_in[load], 16)

        @block.gpsimd
        def _(pool):
            pool.iota(rows_iota[:, :, :], pattern=[[1, P], [0, PAIR]], base=0, channel_multiplier=0,
                      allow_small_or_imprecise_dtypes=True).then_inc(iotas, 1)
            pool.iota(codes_iota[:, :], pattern=[[1, CODES]], base=BASE, channel_multiplier=0,
                      allow_small_or_imprecise_dtypes=True).then_inc(iotas, 1)
            pool.iota(own[:, :], pattern=[[1, NW], [0, WT]], base=0, channel_multiplier=0,
                      allow_small_or_imprecise_dtypes=True).then_inc(iotas, 1)

        @block.vector
        def _(dve):
            chain = Chain(dve, dve_chain)
            dve.memset(zeros[:, :], 0.0).then_inc(zeros_ready, 1)
            chain(dve.memset(k.ADJ[:, :, NW * W:NP], 0.0))
            dve.sem_inc(counted, RING)
            dve.wait_ge(iotas, 3)
            lo, mid, hi = low_i[:, 0, :], low_i[:, 1, :], low_i[:, 2, :]
            for load in range(LOADS):
                at = slice(load * lcol, (load + 1) * lcol)
                keys = window_keys[:, at]
                dve.wait_ge(window_in[load], 16 * LW)
                chain(dve.tensor_scalar(lo, keys, P - 1, None, ALU.bitwise_and))
                chain(dve.tensor_copy(row[:, at], lo))
                chain(dve.tensor_scalar(lo, keys, 3, 0x1F0, ALU.logical_shift_right, ALU.bitwise_and))
                chain(dve.tensor_scalar(mid, keys, SRC_BITS, W - 1, ALU.logical_shift_right, ALU.bitwise_and))
                chain(dve.tensor_scalar(hi, keys, SRC_BITS + 4, None, ALU.logical_shift_right))
                chain(dve.tensor_tensor(code[:, at], lo, mid, ALU.add))
                chain(dve.tensor_tensor(inside[:, at], hi, own[:, at], ALU.is_equal))
                chain(nc.vector.scalar_tensor_tensor(out=code[:, at], in0=inside[:, at], scalar=float(BASE), in1=code[:, at],
                                                     op0=ALU.mult, op1=ALU.add))
                dve.tensor_scalar(negative[:, load * LW:(load + 1) * LW], code[:, at].rearrange("p (w j) -> p w j", j=WT)[:, :, WT - 1],
                                  -1.0, None, ALU.mult).then_inc(codes_ready, 1)
                with dve.Fori(0, LW // RING) as r:
                    for b in range(RING):
                        w = r * RING + (load * LW + b)
                        if b % 2 == 0:
                            dve.wait_ge(counted, w + 2)
                            dve.tensor_tensor(hot_row[:, b // 2, :, :], rows_iota[:, :, :],
                                              row[:, bass.ds(w * WT, PAIR)].unsqueeze(1).to_broadcast([P, P, PAIR]), ALU.is_equal)
                        for j in range(WT - 1):
                            col = bass.ds(w * WT + j, 1)
                            last = dve.tensor_scalar(hot_code[:, b, j, :], codes_iota[:, :], code[:, col], None, ALU.is_equal)
                        last.then_inc(hot_ready, 1)
            dve.tensor_reduce(inside_sum[:, :], inside[:, :], axis=AX, op=ALU.add).then_inc(sum_ready, 1)
            dve.wait_ge(degree_ready, 1)
            chain(dve.tensor_reduce(k.out_deg[:, :], degree_ps[:, 0:CODES].rearrange("p (t w) -> p t w", w=W), axis=AX, op=ALU.add))
            dve.wait_ge(total_ready, 1)
            dve.tensor_scalar(missed[:, :], total_ps[0:1, 0:1], float(E), None, ALU.is_lt).then_inc(flag_ready, 1)
            dve.wait_ge(flag_ready, 1)
            again = dve.value_load(missed[0:1, 0:1], min_val=0, max_val=1)
            with dve.If(again):
                dve.sem_inc(g_counted, RING)
                dve.wait_ge(g_keys_in, 16)
                for at in range(0, EF, lcol):
                    n = min(lcol, EF - at)
                    keys, lo, mid = window_keys[0:EP, at:at + n], low_i[0:EP, 0, 0:n], low_i[0:EP, 1, 0:n]
                    chain(dve.tensor_scalar(lo, keys, P - 1, None, ALU.bitwise_and))
                    chain(dve.tensor_copy(row[0:EP, at:at + n], lo))
                    chain(dve.tensor_scalar(lo, keys, 3, 0x1F0, ALU.logical_shift_right, ALU.bitwise_and))
                    chain(dve.tensor_scalar(mid, keys, SRC_BITS, W - 1, ALU.logical_shift_right, ALU.bitwise_and))
                    chain(dve.tensor_tensor(g_place[:, at:at + n], lo, mid, ALU.add))
                    chain(dve.tensor_scalar(lo, keys, SRC_BITS + 4, None, ALU.logical_shift_right))
                    chain(dve.tensor_copy(g_window[:, at:at + n], lo))
                chain(dve.memset(this_window[:, :], 0.0))
                with dve.Fori(0, NW) as w:
                    chain.loop(w, 3)
                    dve.wait_ge(g_counted, w * batches + RING)
                    chain.all()
                    chain(dve.tensor_scalar(g_code, g_window, this_window[0:EP, :], float(BASE), ALU.is_equal, ALU.mult))
                    chain(dve.tensor_tensor(g_code, g_code, g_place, ALU.add))
                    chain.later(dve.tensor_scalar(this_window[:, :], this_window[:, :], 1.0, None, ALU.add))
                    with dve.Fori(0, batches // RING) as r:
                        for b in range(RING):
                            if b % 2 == 0:
                                dve.wait_ge(g_counted, w * batches + r * RING + (b + 2))
                                dve.tensor_tensor(hot_row[0:EP, b // 2, :, :], rows_iota[0:EP, :, :],
                                                  row[0:EP, bass.ds(r * RING * WT + b * WT, PAIR)].unsqueeze(1).to_broadcast([EP, P, PAIR]),
                                                  ALU.is_equal)
                            for j in range(WT):
                                last = dve.tensor_scalar(hot_code[0:EP, b, j, :], codes_iota[0:EP, :],
                                                         code[0:EP, bass.ds(r * RING * WT + (b * WT + j), 1)], None, ALU.is_equal)
                            last.then_inc(g_hot_ready, 1)
                chain.end(NW)
                dve.wait_ge(g_degree_ready, 1)
                chain(dve.tensor_reduce(k.out_deg[:, :], degree_ps[:, 0:CODES].rearrange("p (t w) -> p t w", w=W), axis=AX,
                                        op=ALU.add))

        @block.tensor
        def _(pe):
            pe.wait_ge(zeros_ready, 1)
            pe.wait_ge(iotas, 3)

            def window(w, b):
                pe.wait_ge(hot_ready, w + 1)
                pe.wait_ge(act_hot_ready, w + 1)
                pe.wait_ge(stored, w + 1)
                for j in range(WT):
                    last = nc.tensor.matmul(counts[:, b, 0:CODES], hot_row[:, b // 2, :, b % 2 * WT + j], hot_code[:, b, j, :],
                                            start=j == 0, stop=j == WT - 1)
                last.then_inc(counted, 1)

            def degree(w, stop=False):
                pe.wait_ge(stored, RING + 1 + w)
                return nc.tensor.matmul(degree_ps[:, 0:CODES], k.ident_h[:, :],
                                        k.ADJ[:, :, bass.ds(w * W, W)], start=False, stop=stop)

            nc.tensor.matmul(degree_ps[:, 0:CODES], zeros[:, :],
                             flat(rows_iota[:, :, :])[:, 0:CODES], start=True, stop=False)
            for b in range(RING):
                window(b, b)
            with pe.Fori(1, rounds) as r:
                for b in range(RING):
                    window(r * RING + b, b)
                    degree(r * RING + (b - RING))
            for b in range(RING):
                last = degree(NW - RING + b, stop=b == RING - 1)
            last.then_inc(degree_ready, 1)
            pe.wait_ge(sum_ready, 1)
            nc.tensor.matmul(total_ps[0:1, 0:1], inside_sum[:, :], k.ones[:, 0:1], start=True, stop=True).then_inc(total_ready, 1)
            pe.wait_ge(flag_ready, 1)
            again = pe.value_load(missed[0:1, 0:1], min_val=0, max_val=1)
            with pe.If(again):
                def clear(out, stop=False):
                    return nc.tensor.matmul(out, zeros[:, :], flat(rows_iota[:, :, :])[:, 0:CODES], start=not stop, stop=stop)

                clear(degree_ps[:, 0:CODES])
                with pe.Fori(0, NW) as w:
                    pe.wait_ge(g_stored, w + 1)
                    clear(counts[:, 0, 0:CODES])
                    with pe.Fori(0, batches // RING) as r:
                        for b in range(RING):
                            pe.wait_ge(g_hot_ready, w * batches + r * RING + (b + 1))
                            for j in range(WT):
                                last = nc.tensor.matmul(counts[:, 0, 0:CODES], hot_row[0:EP, b // 2, :, b % 2 * WT + j], hot_code[0:EP, b, j, :],
                                                        start=False, stop=False)
                            last.then_inc(g_counted, 1)
                    clear(counts[:, 0, 0:CODES], stop=True).then_inc(g_window_done, 1)
                    pe.wait_ge(g_stored, w + 2)
                    nc.tensor.matmul(degree_ps[:, 0:CODES], k.ident_h[:, :], k.ADJ[:, :, bass.ds(w * W, W)], start=False,
                                     stop=False)
                clear(degree_ps[:, 0:CODES], stop=True).then_inc(g_degree_ready, 1)

        @block.scalar
        def _(act):
            act.preload_act_table(ACT.Copy)
            act.sem_inc(stored, RING)
            load_windows(act, 0, LW // 2, LW // 2 // LOADS_AT_ONCE)

            def distances(w, b, first=False):
                if not first:
                    act.wait_ge(act_hot_ready, w - 2 - b % 2)
                nc.scalar.activation(distance[:, b, :], codes_iota[:, :], ACT.Abs,
                                     bias=negative[:, bass.ds(w, 1)]).then_inc(distance_ready, 1)

            def one_hot(w, b):
                act.wait_ge(counted, w + 1)
                act.wait_ge(distance_ready, w + 1)
                nc.scalar.activation(hot_code[:, b - 1:b + 1, WT - 1, :], distance[:, b - 1:b + 1, :], ACT.Relu, scale=-1.0,
                                     bias=1.0).then_inc(act_hot_ready, 2)

            def store(w, b):
                act.wait_ge(counted, RING + 2 + w)
                nc.scalar.activation(k.ADJ[:, :, bass.ds(w * W, 2 * W)].rearrange("p t (b w) -> p b t w", w=W),
                                     counts[:, b:b + 2, 0:CODES].rearrange("p b (t w) -> p b t w", w=W),
                                     ACT.Copy).then_inc(stored, 2)

            act.wait_ge(iotas, 3)
            for load in range(LOADS):
                act.wait_ge(codes_ready, load + 1)
                if load == 0:
                    for b in range(RING):
                        distances(b, b, first=True)
                        if b == STORE_BEHIND:
                            store(0, 0)
                        if b % 2 == 1:
                            one_hot(b, b)
                with act.Fori(1 if load == 0 else 0, LW // RING) as r:
                    for b in range(RING):
                        w = r * RING + (load * LW + b)
                        distances(w, b)
                        if b % 2 == 1:
                            one_hot(w, b)
                            store(r * RING + (load * LW + b - STORE_BEHIND), (b - STORE_BEHIND) % RING)
            store(NW - 2, RING - 2)
            act.wait_ge(stored, RING + NW)
            act.wait_ge(flag_ready, 1)
            again = act.value_load(missed[0:1, 0:1], min_val=0, max_val=1)
            with act.If(again):
                act.sem_inc(g_stored, 1)
                with act.Fori(0, NW) as w:
                    act.wait_ge(g_window_done, w + 1)
                    nc.scalar.activation(k.ADJ[:, :, bass.ds(w * W, W)],
                                         counts[:, 0, 0:CODES].rearrange("p (t w) -> p t w", w=W),
                                         ACT.Copy).then_inc(g_stored, 1)
                act.wait_ge(g_stored, NW + 1)

        @block.sync
        def _(sp):
            load_windows(sp, 0, 0, LW // 2 // LOADS_AT_ONCE)
            for load in range(1, LOADS):
                load_windows(sp, load, 0, LW // LOADS_AT_ONCE)
            sp.wait_ge(flag_ready, 1)
            again = sp.value_load(missed[0:1, 0:1], min_val=0, max_val=1)
            with sp.If(again):
                sp.dma_start(window_keys[0:EP, 0:EF], d.keys.rearrange("(p f) -> p f", p=EP)).then_inc(g_keys_in, 16)
                sp.wait_ge(g_keys_in, 16)


PARTS = 2
SCALE = 2048.0
ONE = PARTS * C
YC = ONE + 2
CHUNK = 4
CW = CHUNK * P
BIG = 3.0e38
BN_EPS = GN_EPS = 1e-5


def tiles(ap, g, n=G):
    return ap[:, g * n:(g + 1) * n, :] if isinstance(g, int) else ap[:, bass.ds(g * n, n), :]


def group(ap, g):
    return ap[:, g * G:(g + 1) * G]


def across(ap):
    return ap.unsqueeze(2).to_broadcast([P, ap.shape[1], C])


def down(ap, n=NT):
    return ap.unsqueeze(1).to_broadcast([P, n, C])


def part(k, q, g):
    return tiles(k.Y, g)[:, :, q * C:(q + 1) * C]


def pe_aggregate(k, nc, pe, s, reads, cols, after):
    def product(j, i):
        return nc.tensor.matmul(k.ps[:, j % G, 0:cols], k.ADJ[:, i, j * P:(j + 1) * P], k.Y[:, i, 0:cols],
                                start=i == 0, stop=i == NT - 1)

    for g in range(NG):
        pe.wait_ge(s.y_ready, g + 1)
        for j in range(G):
            for i in range(g * G, (g + 1) * G):
                last = product(j, i)
            if g == NG - 1:
                last.then_inc(s.summed, 1)
    for j in range(NT):
        if j >= G:
            pe.wait_ge(s.emptied, (j + 1 - G) * reads)
            for i in range(NT):
                last = product(j, i)
            last.then_inc(s.summed, 1)
        after(j)


def add_parts(nc, k, out, b):
    return nc.vector.tensor_reduce(out, k.ps[:, b, 0:ONE].rearrange("p (q f) -> p f q", q=PARTS), axis=AX, op=ALU.add)


def unscaled(nc, k, factor, g):
    return nc.vector.scalar_tensor_tensor(out=tiles(k.H, g), in0=tiles(k.H, g), scalar=1 / SCALE, in1=across(group(factor, g)),
                                          op0=ALU.mult, op1=ALU.mult)


def act_high(nc, k, g, high):
    nc.scalar.activation(part(k, 0, g), tiles(k.H, g), ACT.Copy, scale=SCALE).then_inc(high, 1)


def dve_low(nc, k, dve, g, high, y_ready):
    dve.wait_ge(high, g + 1)
    nc.vector.scalar_tensor_tensor(out=part(k, 1, g), in0=tiles(k.H, g), scalar=SCALE, in1=part(k, 0, g), op0=ALU.mult,
                                   op1=ALU.subtract).then_inc(y_ready, 1)



def dve_centre(nc, k, dve, chain, g, centred):
    mean = group(k.s1, g)
    chain(dve.tensor_reduce(mean, tiles(k.X, g), axis=AX, op=ALU.add))
    chain(dve.tensor_scalar(mean, mean, 1.0 / C, None, ALU.mult))
    dve.tensor_tensor(tiles(k.H, g), tiles(k.X, g), across(mean), ALU.subtract).then_inc(centred, 1)


def act_square(nc, k, act, g, centred, squared, read):
    act.wait_ge(centred, g + 1)
    if g >= 2:
        act.wait_ge(read, g - 1)
    nc.scalar.activation(k.T2[:, g % 2, :, :], tiles(k.H, g), ACT.Square).then_inc(squared, 1)


def dve_square_sum(k, dve, g, squared, read):
    dve.wait_ge(squared, g + 1)
    dve.tensor_reduce(group(k.s2, g), k.T2[:, g % 2, :, :], axis=AX, op=ALU.add).then_inc(read, 1)


def dve_normalise(nc, k, dve, chain, read, variance, deviation, done):
    dve.wait_ge(read, NG)
    dve.tensor_scalar(k.s1[:, :], k.s2[:, :], 1.0 / C, LN_EPS, ALU.mult, ALU.add).then_inc(variance, 1)
    dve.wait_ge(deviation, 1)
    chain(dve.reciprocal(k.s2[:, :], k.s2[:, :]))
    for g in range(NG):
        nc.vector.scalar_tensor_tensor(out=tiles(k.H, g), in0=tiles(k.H, g), scalar=0.0, in1=across(group(k.s2, g)),
                                       op0=ALU.max, op1=ALU.mult).then_inc(done, 1)


def act_deviation(nc, k, act, variance, deviation):
    act.wait_ge(variance, 1)
    nc.scalar.activation(k.s2[:, :], k.s1[:, :], ACT.Sqrt).then_inc(deviation, 1)


def pe_column_sums(nc, k, pe, ready, of, out, g):
    pe.wait_ge(ready, g + 1)
    for t in range(g * G, (g + 1) * G):
        rows = P if t < NT - 1 else LAST
        last = nc.tensor.matmul(out, k.ones[0:rows, :], of[0:rows, t, :], start=t == 0, stop=t == NT - 1)
    return last


def load_rows(sp, loads, done):
    for to, of in loads:
        if len(of.shape) == 1:
            of = of.rearrange("(a f) -> a f", a=1).to_broadcast([P, C])
        sp.dma_start(to[:, :], of).then_inc(done, 16)


def convolutions(nc, k, d):
    with ExitStack() as c:
        s = semaphores(nc, k, "c1", "chain vectors centred squared read variance deviation normal clipped root value high "
                       "y_ready summed emptied in_clipped in_root h_ready sums_ready centred_h squared_h squares_ready "
                       "var_h dev_h scaled affine gated")
        u = semaphores(nc, k, "c2", "value high y_ready summed emptied centred squared read variance deviation normal")
        bias, bias2, gamma, beta, mean, scale, shift = (
            c.enter_context(nc.sbuf_tensor(f"c1_{n}", [P, C], F32)) for n in "bias bias2 gamma beta mean scale shift".split())
        block = c.enter_context(nc.Block())
        sums, squares = k.ps[:, 5, 0:C], k.ps[:, 6, 0:C]

        @block.sync
        def _(sp):
            load_rows(sp, [(bias, d.bias1), (gamma, d.gamma), (beta, d.beta), (bias2, d.bias2)], s.vectors)
            sp.wait_ge(s.vectors, 4 * 16)

        @block.vector
        def _(dve):
            chain = Chain(dve, s.chain)
            dve.tensor_scalar(k.s3[:, :], k.out_deg[:, :], 1.0, None, ALU.max).then_inc(s.clipped, 1)
            for g in range(NG):
                dve_centre(nc, k, dve, chain, g, s.centred)
                if g >= 1:
                    dve_square_sum(k, dve, g - 1, s.squared, s.read)
            dve.wait_ge(s.root, 1)
            chain(dve.reciprocal(k.out_norm[:, :], k.out_norm[:, :]))
            chain(nc.vector.scalar_tensor_tensor(out=k.dis[:, :], in0=k.out_deg[:, :], scalar=1.0, in1=k.out_norm[:, :],
                                                 op0=ALU.min, op1=ALU.mult))
            chain(dve.memset(k.Y[:, :, ONE:YC], 1.0))
            dve_square_sum(k, dve, NG - 1, s.squared, s.read)
            dve.wait_ge(s.read, NG)
            dve.tensor_scalar(k.s1[:, :], k.s2[:, :], 1.0 / C, LN_EPS, ALU.mult, ALU.add).then_inc(s.variance, 1)
            dve.wait_ge(s.deviation, 1)
            chain(dve.reciprocal(k.s2[:, :], k.s2[:, :]))
            chain(dve.tensor_tensor(k.s2[:, :], k.s2[:, :], k.out_norm[:, :], ALU.mult))
            for g in range(NG):
                nc.vector.scalar_tensor_tensor(out=tiles(k.H, g), in0=tiles(k.H, g), scalar=0.0, in1=across(group(k.s2, g)),
                                               op0=ALU.max, op1=ALU.mult).then_inc(s.value, 1)
                if g >= 1:
                    dve_low(nc, k, dve, g - 1, s.high, s.y_ready)
            dve_low(nc, k, dve, NG - 1, s.high, s.y_ready)

            def degrees(g):
                dve.wait_ge(s.emptied, 2 * G * (g + 1))
                chain(dve.tensor_scalar(group(k.in_deg, g), group(k.in_deg, g), 1.0, None, ALU.max))
                dve.reciprocal(group(k.inv_deg, g), group(k.in_deg, g)).then_inc(s.in_clipped, 1)

            def finish(g):
                dve.wait_ge(s.in_root, g + 1)
                chain(dve.reciprocal(group(k.in_norm, g), group(k.in_norm, g)))
                chain(unscaled(nc, k, k.in_norm, g))
                dve.tensor_tensor(tiles(k.H, g), tiles(k.H, g), down(bias[:, :], G), ALU.add).then_inc(s.h_ready, 1)

            dve.wait_ge(s.vectors, 4 * 16)
            for j in range(NT):
                dve.wait_ge(s.summed, j + 1)
                add_parts(nc, k, tiles(k.H, j, 1), j % G).then_inc(s.emptied, 1)
                nc.vector.tensor_copy(k.in_deg[:, j:j + 1], k.ps[:, j % G, ONE:ONE + 1]).then_inc(s.emptied, 1)
                if j % G == G - 1:
                    degrees(j // G)
                if j % G == 1 and j > G:
                    finish(j // G - 1)
            finish(NG - 1)
            dve.wait_ge(s.sums_ready, 1)
            chain(dve.tensor_scalar(mean[:, :], sums, 1.0 / N, None, ALU.mult))
            for g in range(NG):
                dve.tensor_tensor(tiles(k.H, g), tiles(k.H, g), down(mean[:, :], G), ALU.subtract).then_inc(s.centred_h, 1)
            dve.wait_ge(s.squares_ready, 1)
            dve.tensor_scalar(scale[:, :], squares, 1.0 / N, BN_EPS, ALU.mult, ALU.add).then_inc(s.var_h, 1)
            dve.wait_ge(s.dev_h, 1)
            chain(dve.reciprocal(scale[:, :], shift[:, :]))
            chain(dve.tensor_tensor(scale[:, :], scale[:, :], gamma[:, :], ALU.mult))

            def scaled(g):
                dve.tensor_tensor(tiles(k.H, g), tiles(k.H, g), down(scale[:, :], G), ALU.mult).then_inc(s.scaled, 1)

            scaled(0)
            for g in range(NG):
                if g + 1 < NG:
                    scaled(g + 1)
                dve.wait_ge(s.scaled, g + 1)
                dve.tensor_tensor(tiles(k.H, g), tiles(k.H, g), down(beta[:, :], G), ALU.add).then_inc(s.affine, 1)
            for g in range(NG):
                dve_low(nc, k, dve, g, u.high, u.y_ready)

            def residual(g):
                dve.wait_ge(u.emptied, G * (g + 1))
                chain(unscaled(nc, k, k.in_norm, g))
                chain(dve.tensor_tensor(tiles(k.H, g), tiles(k.H, g), down(bias2[:, :], G), ALU.add))
                chain(dve.tensor_tensor(tiles(k.X, g), tiles(k.X, g), tiles(k.H, g), ALU.add))
                dve_centre(nc, k, dve, chain, g, u.centred)
                if g >= 1:
                    dve_square_sum(k, dve, g - 1, u.squared, u.read)

            for j in range(NT):
                dve.wait_ge(u.summed, j + 1)
                add_parts(nc, k, tiles(k.H, j, 1), j % G).then_inc(u.emptied, 1)
                if j % G == G - 1:
                    residual(j // G)
            dve_square_sum(k, dve, NG - 1, u.squared, u.read)
            dve_normalise(nc, k, dve, chain, u.read, u.variance, u.deviation, u.normal)

        @block.gpsimd
        def _(pool):
            for g in range(NG):
                pool.wait_ge(s.gated, g + 1)
                pool.tensor_tensor(tiles(k.H, g), tiles(k.H, g), across(group(k.out_norm, g)), ALU.mult).then_inc(u.value, 1)

        @block.scalar
        def _(act):
            act.wait_ge(s.clipped, 1)
            nc.scalar.activation(k.out_norm[:, :], k.s3[:, :], ACT.Sqrt).then_inc(s.root, 1)
            for g in range(NG):
                act_square(nc, k, act, g, s.centred, s.squared, s.read)
            act_deviation(nc, k, act, s.variance, s.deviation)
            for g in range(NG):
                act.wait_ge(s.value, g + 1)
                act_high(nc, k, g, s.high)
            for g in range(NG):
                act.wait_ge(s.in_clipped, g + 1)
                nc.scalar.activation(group(k.in_norm, g), group(k.in_deg, g), ACT.Sqrt).then_inc(s.in_root, 1)
            for g in range(NG):
                act.wait_ge(s.centred_h, g + 1)
                nc.scalar.activation(tiles(k.T, g), tiles(k.H, g), ACT.Square).then_inc(s.squared_h, 1)
            act.wait_ge(s.var_h, 1)
            nc.scalar.activation(shift[:, :], scale[:, :], ACT.Sqrt).then_inc(s.dev_h, 1)
            for g in range(NG):
                act.wait_ge(s.affine, g + 1)
                nc.scalar.activation(tiles(k.H, g), tiles(k.H, g), ACT.Sigmoid).then_inc(s.gated, 1)
            for g in range(NG):
                act.wait_ge(u.value, g + 1)
                act_high(nc, k, g, u.high)
            for g in range(NG):
                act_square(nc, k, act, g, u.centred, u.squared, u.read)
            act_deviation(nc, k, act, u.variance, u.deviation)

        @block.tensor
        def _(pe):
            def column_sums(j):
                if j % G == G - 2 and j > G:
                    pe_column_sums(nc, k, pe, s.h_ready, k.H, sums, j // G - 1)

            pe_aggregate(k, nc, pe, s, 2, ONE + 1, column_sums)
            pe_column_sums(nc, k, pe, s.h_ready, k.H, sums, NG - 1).then_inc(s.sums_ready, 1)
            for g in range(NG):
                last = pe_column_sums(nc, k, pe, s.squared_h, k.T, squares, g)
            last.then_inc(s.squares_ready, 1)
            pe_aggregate(k, nc, pe, u, 1, ONE, lambda j: None)


def sage(nc, k, d):
    with ExitStack() as c:
        names = "high y_ready summed emptied scaled_a agg_ready turned copied product added "
        s = semaphores(nc, k, "sg1", names + "chain vectors inputs parts_ready total_ready bound bound_root weights relu")
        u = semaphores(nc, k, "sg2", names + "biased centred squared read variance deviation normal stored")
        w1, w2 = (c.enter_context(nc.sbuf_tensor(f"sg_w{n}", [C, 2 * C], F32)) for n in (1, 2))
        b1, b2 = (c.enter_context(nc.sbuf_tensor(f"sg_b{n}", [P, C], F32)) for n in (1, 2))
        b1_column = c.enter_context(nc.sbuf_tensor("sg_b1_column", [C, 1], F32))
        w_squares = c.enter_context(nc.sbuf_tensor("sg_w_squares", [C, 2 * C], F32))
        parts = c.enter_context(nc.sbuf_tensor("sg_parts", [C, 2], F32))
        size = c.enter_context(nc.sbuf_tensor("sg_size", [P, 4], F32))
        A = c.enter_context(nc.sbuf_tensor("sg_sum", [P, 3, C], F32))
        HT = c.enter_context(nc.sbuf_tensor("sg_turned", [C, 2, 2 * P], F32))
        block = c.enter_context(nc.Block())
        TURNED, PRODUCT = 5, 6

        @block.sync
        def _(sp):
            sp.dma_start(w1[:, 0:C], d.W_neigh1).then_inc(s.inputs, 16)
            sp.dma_start(w1[:, C:2 * C], d.W_self1).then_inc(s.inputs, 16)
            sp.dma_start(b1_column[:, :], d.b1.rearrange("(f a) -> f a", a=1)).then_inc(s.inputs, 16)
            load_rows(sp, [(b1, d.b1), (b2, d.b2)], s.inputs)
            sp.dma_start(w2[:, 0:C], d.W_neigh2).then_inc(s.inputs, 16)
            sp.dma_start(w2[:, C:2 * C], d.W_self2).then_inc(s.inputs, 16)
            for g in range(NG):
                sp.wait_ge(u.normal, g + 1)
                sp.dma_start(tiles(d.residual, g), tiles(k.H, g)).then_inc(u.stored, 16)
            sp.wait_ge(s.inputs, 7 * 16)
            sp.wait_ge(u.stored, NG * 16)

        @block.vector
        def _(dve):
            chain = Chain(dve, s.chain)
            for g in range(NG):
                dve_low(nc, k, dve, g, s.high, s.y_ready)
            dve.wait_ge(s.inputs, 7 * 16)
            chain(dve.tensor_tensor(w_squares[:, :], w1[:, :], w1[:, :], ALU.mult))
            chain(dve.tensor_reduce(parts[:, 0:1], w_squares[:, :], axis=AX, op=ALU.add))
            chain(dve.tensor_tensor(parts[:, 1:2], b1_column[:, :], b1_column[:, :], ALU.mult))
            nc.vector.scalar_tensor_tensor(out=parts[:, 0:1], in0=parts[:, 0:1], scalar=2.0 * C, in1=parts[:, 1:2],
                                           op0=ALU.mult, op1=ALU.add).then_inc(s.parts_ready, 1)
            dve.wait_ge(s.total_ready, 1)
            dve.tensor_scalar(size[:, 0:1], k.ps[:, PRODUCT, 0:1], 2.0, 1e-30, ALU.mult, ALU.add).then_inc(s.bound, 1)
            dve.wait_ge(s.bound_root, 1)
            chain(dve.reciprocal(size[:, 2:3], size[:, 1:2]))
            chain(dve.tensor_scalar(b1[:, :], b1[:, :], size[:, 2:3], None, ALU.mult))
            dve.tensor_scalar(w1[:, :], w1[:, :], size[0:C, 2:3], None, ALU.mult).then_inc(s.weights, 1)
            dve.tensor_scalar(w2[:, :], w2[:, :], size[0:C, 1:2], None, ALU.mult).then_inc(s.weights, 1)

            def mean_of(j, v):
                out = A[:, j % 3, :]
                dve.wait_ge(v.summed, j + 1)
                if j >= 3:
                    dve.wait_ge(v.turned, j - 2)
                add_parts(nc, k, A[:, j % 3:j % 3 + 1, :], j % G).then_inc(v.emptied, 1)
                dve.wait_ge(v.emptied, j + 1)
                dve.tensor_scalar(out, out, k.inv_deg[:, j:j + 1], 1 / SCALE, ALU.mult, ALU.mult).then_inc(v.agg_ready, 1)

            def output_1(j):
                dve.wait_ge(s.product, j + 1)
                dve.tensor_tensor(k.H[:, j, :], k.ps[:, PRODUCT + j % 2, 0:C], b1[:, :], ALU.add).then_inc(s.added, 1)

            for j in range(NT + 2):
                if j < NT:
                    mean_of(j, s)
                if j >= 2:
                    output_1(j - 2)
            for g in range(NG):
                dve_low(nc, k, dve, g, u.high, u.y_ready)
            dve.tensor_tensor(k.X[:, :, :], k.X[:, :, :], down(b2[:, :]), ALU.add).then_inc(u.biased, 1)
            dve.wait_ge(u.biased, 1)

            def output_2(j):
                dve.wait_ge(u.product, j + 1)
                dve.tensor_tensor(k.X[:, j, :], k.X[:, j, :], k.ps[:, PRODUCT + j % 2, 0:C], ALU.add).then_inc(u.added, 1)
                if j % G == G - 1:
                    g = j // G
                    dve.wait_ge(u.added, j + 1)
                    dve_centre(nc, k, dve, chain, g, u.centred)
                    if g >= 1:
                        dve_square_sum(k, dve, g - 1, u.squared, u.read)

            for j in range(NT + 2):
                if j < NT:
                    mean_of(j, u)
                if j >= 2:
                    output_2(j - 2)
            dve_square_sum(k, dve, NG - 1, u.squared, u.read)
            dve_normalise(nc, k, dve, chain, u.read, u.variance, u.deviation, u.normal)

        @block.scalar
        def _(act):
            for g in range(NG):
                act_high(nc, k, g, s.high)
            act.wait_ge(s.bound, 1)
            nc.scalar.activation(size[:, 1:2], size[:, 0:1], ACT.Sqrt).then_inc(s.bound_root, 1)

            def copy_turned(j, v):
                act.wait_ge(v.turned, j + 1)
                if j >= 2:
                    act.wait_ge(v.product, j - 1)
                nc.scalar.activation(HT[:, j % 2, :], k.ps[0:C, TURNED, 0:2 * P], ACT.Copy).then_inc(v.copied, 1)

            def relu(g):
                act.wait_ge(s.added, G * (g + 1))
                nc.scalar.activation(tiles(k.H, g), tiles(k.H, g), ACT.Relu).then_inc(s.relu, 1)

            for j in range(NT):
                copy_turned(j, s)
                if j % G == 3 and j > G:
                    relu(j // G - 1)
            relu(NG - 1)
            act.wait_ge(s.summed, NT)
            act.wait_ge(s.relu, NG)
            for g in range(NG):
                act_high(nc, k, g, u.high)
            for j in range(NT):
                copy_turned(j, u)
                if j % G == 4 and j > G:
                    act_square(nc, k, act, j // G - 1, u.centred, u.squared, u.read)
            act_square(nc, k, act, NG - 1, u.centred, u.squared, u.read)
            act_deviation(nc, k, act, u.variance, u.deviation)

        @block.tensor
        def _(pe):
            def turn(j, v):
                pe.wait_ge(v.agg_ready, j + 1)
                if j >= 1:
                    pe.wait_ge(v.copied, j)
                nc.tensor.transpose(k.ps[0:C, TURNED, 0:P], A[:, j % 3, :], k.ident[:, :])
                nc.tensor.transpose(k.ps[0:C, TURNED, P:2 * P], k.H[:, j, :], k.ident[:, :]).then_inc(v.turned, 1)

            def multiply(j, v, w):
                pe.wait_ge(v.copied, j + 1)
                if j >= 2:
                    pe.wait_ge(v.added, j - 1)
                bank = k.ps[:, PRODUCT + j % 2, 0:C]
                nc.tensor.matmul(bank, HT[:, j % 2, 0:P], w[:, 0:C], start=True, stop=False)
                nc.tensor.matmul(bank, HT[:, j % 2, P:2 * P], w[:, C:2 * C], start=False, stop=True).then_inc(v.product, 1)

            def step(v, w):
                def after(j):
                    if j == 0 and v is s:
                        pe.wait_ge(s.parts_ready, 1)
                        nc.tensor.matmul(k.ps[:, PRODUCT, 0:1], k.ones[0:C, :], parts[:, 0:1], start=True,
                                         stop=True).then_inc(s.total_ready, 1)
                    if 1 <= j <= NT:
                        turn(j - 1, v)
                    if j == 2 and v is s:
                        pe.wait_ge(s.weights, 2)
                    if j >= 2:
                        multiply(j - 2, v, w)
                return after

            for v, w in ((s, w1), (u, w2)):
                after = step(v, w)
                pe_aggregate(k, nc, pe, v, 1, ONE, after)
                after(NT)
                after(NT + 1)


def prepare_attention(nc, k, d, name, w, a_src, a_dst, first):
    with ExitStack() as c:
        s = semaphores(nc, k, name, "chain loads w_turned w_copied v_ready weights turned copied product emptied_d "
                       "extremes ex_turned ex_diag ex_rows")
        w_in = c.enter_context(nc.sbuf_tensor(f"{name}_w", [C, C], F32))
        a_in = c.enter_context(nc.sbuf_tensor(f"{name}_a", [C, 2], F32))
        weights = c.enter_context(nc.sbuf_tensor(f"{name}_weights", [C, C + 2], F32))
        ext = c.enter_context(nc.sbuf_tensor(f"{name}_ext", [P, 8], F32))
        HT = c.enter_context(nc.sbuf_tensor(f"{name}_HT", [C, 2, G * P], F32))

        def turned_banks(g):
            return flat(k.ps[0:C, g % 2 * 2:g % 2 * 2 + 2, :])[:, 0:G * P]

        block = c.enter_context(nc.Block())

        @block.sync
        def _(sp):
            sp.dma_start(w_in[:, :], w).then_inc(s.loads, 16)
            sp.dma_start(a_in[:, 0:1], a_src.rearrange("(f a) -> f a", a=1)).then_inc(s.loads, 16)
            sp.dma_start(a_in[:, 1:2], a_dst.rearrange("(f a) -> f a", a=1)).then_inc(s.loads, 16)
            sp.wait_ge(s.loads, 48)

        @block.vector
        def _(dve):
            chain = Chain(dve, s.chain)
            if first:
                adj = flat(k.ADJ[:, :, :])
                most = adj[:, 0:(NT - 1) * (NP + P)].rearrange("p (t q) -> p t q", q=NP + P)[:, :, 0:P]
                chain(dve.tensor_tensor(most, most, k.ident_h[:, :].unsqueeze(1).to_broadcast([P, NT - 1, P]), ALU.add))
                end = adj[:, (NT - 1) * (NP + P):NT * NP]
                chain(dve.tensor_tensor(end, end, k.ident_h[:, :], ALU.add))
            dve.wait_ge(s.w_turned, 2)
            dve.tensor_copy(weights[:, 0:C], k.ps[0:C, 6, 0:C]).then_inc(s.w_copied, 1)
            dve.tensor_copy(weights[:, C:C + 2], k.ps[0:C, 7, 0:2]).then_inc(s.w_copied, 1)
            for g in range(NG):
                dve.wait_ge(s.product, g + 1)
                dve.tensor_copy(tiles(k.Hg, g), k.ps[:, 4 + g % 2, 0:G * (C + 2)].rearrange("p (t f) -> p t f", f=C + 2)).then_inc(s.emptied_d, 1)
            dve.wait_ge(s.emptied_d, NG)
            chain(dve.tensor_copy(k.a_s[:, :], k.Hg[:, :, C]))
            chain(dve.tensor_copy(k.a_d[:, :], k.Hg[:, :, C + 1]))
            chain(dve.memset(k.Hg[:, :, C:C + 1], 1.0))
            chain(dve.tensor_scalar(k.a_s5[:, :], k.a_s[:, :], SLOPE, None, ALU.mult))
            chain(dve.tensor_scalar(k.s3[:, :], k.a_s[:, :], -1.0, None, ALU.mult))
            chain(dve.tensor_scalar(k.s2[:, :], k.a_d[:, :], -1.0, None, ALU.mult))
            chain(dve.tensor_tensor(k.s2[:, :], k.s2[:, :], k.a_d[:, :], ALU.max))
            chain(dve.tensor_reduce(ext[:, 0:1], k.a_s[:, :], axis=AX, op=ALU.max))
            chain(dve.tensor_reduce(ext[:, 1:2], k.s3[:, :], axis=AX, op=ALU.max))
            dve.tensor_reduce(ext[:, 2:3], k.s2[:, :], axis=AX, op=ALU.max).then_inc(s.extremes, 1)
            dve.wait_ge(s.ex_turned, 1)
            chain(dve.tensor_reduce(ext[0:3, 3:4], k.ps[0:3, 6, 0:P], axis=AX, op=ALU.max))
            dve.tensor_scalar(ext[0:3, 4:7], k.ident[0:3, 0:3], ext[0:3, 3:4], None, ALU.mult).then_inc(s.ex_diag, 1)
            dve.wait_ge(s.ex_rows, 1)
            chain(dve.tensor_copy(ext[:, 5:7], k.ps[:, 7, 0:2]))
            chain(dve.tensor_tensor(ext[:, 7:8], ext[:, 5:6], ext[:, 6:7], ALU.add))
            chain(dve.tensor_scalar(ext[:, 7:8], ext[:, 7:8], 1e-20, None, ALU.max))
            chain(dve.tensor_scalar(k.unscale[:, 0:1], ext[:, 7:8], 2.0, None, ALU.mult))
            chain(nc.vector.scalar_tensor_tensor(out=k.unscale[:, 1:2], in0=ext[:, 7:8], scalar=-1.0, in1=ext[:, 6:7],
                                                 op0=ALU.mult, op1=ALU.subtract))
            chain(dve.reciprocal(ext[:, 5:6], k.unscale[:, 0:1]))
            chain(dve.tensor_scalar(k.a_unit[:, :], k.a_s[:, :], ext[:, 6:7], ext[:, 5:6], ALU.add, ALU.mult))
            chain(dve.tensor_scalar(k.a_unit[:, :], k.a_unit[:, :], 0.5, None, ALU.add))
            chain(dve.tensor_reduce(ext[0:1, 0:1], k.ps[0:1, 7, 0:3], axis=AX, op=ALU.max))
            chain(dve.tensor_scalar(k.wide[0:1, 0:1], ext[0:1, 0:1], SMALL, None, ALU.is_gt))

        @block.scalar
        def _(act):
            act.preload_act_table(ACT.Copy)
            for g in range(NG):
                act.wait_ge(s.turned, g + 1)
                if g >= 2:
                    act.wait_ge(s.product, g - 1)
                nc.scalar.activation(HT[:, g % 2, :], turned_banks(g), ACT.Copy).then_inc(s.copied, 1)

        @block.tensor
        def _(pe):
            pe.wait_ge(s.loads, 48)
            nc.tensor.transpose(k.ps[0:C, 6, 0:C], w_in[:, :], k.ident[0:C, 0:C]).then_inc(s.w_turned, 1)
            nc.tensor.matmul(k.ps[0:C, 7, 0:2], w_in[:, :], a_in[:, :], start=True, stop=True).then_inc(s.w_turned, 1)

            def turn(g):
                if g >= 2:
                    pe.wait_ge(s.copied, g - 1)
                for t in range(G):
                    last = nc.tensor.transpose(turned_banks(g)[:, t * P:(t + 1) * P], k.H[:, g * G + t, :], k.ident[:, :])
                last.then_inc(s.turned, 1)

            def multiply(g):
                pe.wait_ge(s.copied, g + 1)
                if g == 0:
                    pe.wait_ge(s.w_copied, 2)
                if g >= 2:
                    pe.wait_ge(s.emptied_d, g - 1)
                for t in range(G):
                    last = nc.tensor.matmul(k.ps[:, 4 + g % 2, t * (C + 2):(t + 1) * (C + 2)], HT[:, g % 2, t * P:(t + 1) * P],
                                            weights[:, :], start=True, stop=True)
                last.then_inc(s.product, 1)

            for g in range(NG + 1):
                if g < NG:
                    turn(g)
                if g >= 1:
                    multiply(g - 1)
            pe.wait_ge(s.extremes, 1)
            nc.tensor.transpose(k.ps[0:3, 6, 0:P], ext[:, 0:3], k.ident[:, :]).then_inc(s.ex_turned, 1)
            pe.wait_ge(s.ex_diag, 1)
            nc.tensor.matmul(k.ps[:, 7, 0:3], k.ones[0:3, :], ext[0:3, 4:7], start=True, stop=True).then_inc(s.ex_rows, 1)


SLOPE = 0.2
NC = NT // CHUNK
REST = NT % CHUNK
MAX_STEPS, SHIFT_STEPS = NT, 5
ACC, TURN, ROWS_U, ROWS_V, OUT, OTHER_OUT = 0, 1, 2, 3, 6, 0
EXPS = (4, 5, 7)
SMALL = 30.0
RING4 = [i % 4 if i < NT - 9 else (i - NT + 9) % 3 for i in range(NT)]


def attend(nc, k, d, name):
    with ExitStack() as c:
        s = semaphores(nc, k, name, "chain max_ready max_turned uv_ready diag_ready rows_ready exp_ready prob_ready "
                       "used out_ready out_copied out_turned h_written small")
        t = semaphores(nc, k, name + "b", "factor hg_ready diag_ready rows_ready exp_ready prob_ready used "
                       "out_copied out_turned norm_ready h_written")
        work = c.enter_context(nc.sbuf_tensor(f"{name}_work", [P, 7, CW], F32))
        prob, odd, exp_v, ring = work[:, 0:2, :], work[:, 2, :], work[:, 3:6, :], work[:, 0:4, :]
        out_sb = work[:, 6, :]
        peak = c.enter_context(nc.sbuf_tensor(f"{name}_peak", [P, CHUNK], F32))
        u = c.enter_context(nc.sbuf_tensor(f"{name}_u", [P, CHUNK], F32))
        v = c.enter_context(nc.sbuf_tensor(f"{name}_v", [P, CHUNK], F32))
        rz = c.enter_context(nc.sbuf_tensor(f"{name}_rz", [P, CHUNK], F32))
        block = c.enter_context(nc.Block())
        diag = k.spare[:, 0:2 * CW].rearrange("p (a q) -> p a q", a=2)

        def cols(ch, n):
            return slice(ch * CW, ch * CW + n * P) if isinstance(ch, int) else bass.ds(ch * CW, n * P)

        def nodes(ch, n):
            return slice(ch * CHUNK, ch * CHUNK + n) if isinstance(ch, int) else bass.ds(ch * CHUNK, n)

        def exact_vector(dve):
            chain = Chain(dve, s.chain)

            def maxima(ch, n):
                acc = (k.ps[:, ACC, 0:n * P], odd[:, 0:n * P])
                for i in range(NT):
                    counts = k.ADJ[:, i, cols(ch, n)]
                    if i < 2:
                        chain.lag(dve.tensor_scalar(acc[i], counts, k.a_unit[:, i:i + 1], None, ALU.min))
                    else:
                        chain.lag(nc.vector.scalar_tensor_tensor(out=acc[i % 2], in0=counts, scalar=k.a_unit[:, i:i + 1],
                                                                 in1=acc[i % 2], op0=ALU.min, op1=ALU.max))
                chain.all()
                dve.tensor_tensor(acc[1], acc[0], acc[1], ALU.max).then_inc(s.max_ready, 1)

            def shifts(ch, n):
                dve.wait_ge(s.max_turned, ch + 1)
                ad, pk, uu, vv = k.a_d[:, nodes(ch, n)], peak[:, 0:n], u[:, 0:n], v[:, 0:n]
                chain(dve.tensor_reduce(pk, k.ps[:, TURN, 0:n * P].rearrange("p (b q) -> p b q", q=P), axis=AX, op=ALU.max))
                chain(dve.tensor_scalar(pk, pk, k.unscale[:, 0:1], k.unscale[:, 1:2], ALU.mult, ALU.add))
                chain(dve.tensor_tensor(pk, pk, ad, ALU.add))
                chain(nc.vector.scalar_tensor_tensor(out=pk, in0=pk, scalar=SLOPE, in1=pk, op0=ALU.mult, op1=ALU.max))
                chain(dve.tensor_tensor(uu, ad, pk, ALU.subtract))
                nc.vector.scalar_tensor_tensor(out=vv, in0=ad, scalar=SLOPE, in1=pk, op0=ALU.mult,
                                               op1=ALU.subtract).then_inc(s.uv_ready, 1)

            def larger(ch, i, n):
                e = i % len(EXPS)
                dve.wait_ge(s.exp_ready, ch * NT + (i + 1))
                bank = k.ps[:, EXPS[e], 0:n * P]
                dve.tensor_tensor(bank, bank, exp_v[:, e, 0:n * P], ALU.max).then_inc(s.small, 1)

            def probabilities(ch, first, n):
                larger(ch, 0, n)
                for i in range(NT):
                    if i + 1 < NT:
                        larger(ch, i + 1, n)
                    dve.wait_ge(s.small, ch * NT + (i + 1))
                    if not first or i >= 2:
                        dve.wait_ge(s.used, ch * NT + (i - 1))
                    nc.vector.scalar_tensor_tensor(out=prob[:, i % 2, 0:n * P], in0=k.ps[:, EXPS[i % len(EXPS)], 0:n * P],
                                                   scalar=BIG, in1=k.ADJ[:, i, cols(ch, n)], op0=ALU.min,
                                                   op1=ALU.mult).then_inc(s.prob_ready, 1)

            def write(ch, n):
                dve.wait_ge(s.out_turned, ch + 1)
                sums = k.ps[:, TURN, 0:n * (C + 1)].rearrange("p (b q) -> p b q", q=C + 1)
                chain(dve.reciprocal(rz[:, 0:n], sums[:, :, C]))
                dve.tensor_tensor(k.H[:, nodes(ch, n), :], sums[:, :, 0:C], rz[:, 0:n].unsqueeze(2).to_broadcast([P, n, C]),
                                  ALU.mult).then_inc(s.h_written, 1)

            maxima(0, CHUNK)
            shifts(0, CHUNK)
            maxima(1, CHUNK)
            probabilities(0, True, CHUNK)
            with dve.Fori(0, NC - 2) as r:
                chain.loop(r, MAX_STEPS + SHIFT_STEPS + 1)
                shifts(r + 1, CHUNK)
                maxima(r + 2, CHUNK)
                write(r, CHUNK)
                probabilities(r + 1, False, CHUNK)
            chain.end(NC - 2)
            shifts(NC - 1, CHUNK)
            maxima(NC, REST)
            write(NC - 2, CHUNK)
            probabilities(NC - 1, False, CHUNK)
            shifts(NC, REST)
            write(NC - 1, CHUNK)
            probabilities(NC, False, REST)
            write(NC, REST)
            dve.wait_ge(s.h_written, NC + 1)

        def exact_gpsimd(pool):
            def diagonals(ch, n):
                pool.wait_ge(s.uv_ready, ch + 1)
                for a, of in ((0, u), (1, v)):
                    pool.tensor_tensor(diag[:, a, 0:n * P].rearrange("p (b q) -> p b q", q=P),
                                       k.ident[:, :].unsqueeze(1).to_broadcast([P, n, P]),
                                       of[:, 0:n].unsqueeze(2).to_broadcast([P, n, P]), ALU.mult).then_inc(s.diag_ready, 1)

            with pool.Fori(0, NC) as ch:
                diagonals(ch, CHUNK)
            diagonals(NC, REST)

        def exact_scalar(act):
            def exponentials(ch, first, n):
                act.wait_ge(s.rows_ready, ch + 1)
                for i in range(NT):
                    e = i % len(EXPS)
                    if i >= len(EXPS):
                        act.wait_ge(s.prob_ready, ch * NT + (i + 1 - len(EXPS)))
                    elif not first:
                        act.wait_ge(s.prob_ready, ch * NT)
                    nc.scalar.activation(k.ps[:, EXPS[e], 0:n * P], k.ps[:, ROWS_U, 0:n * P], ACT.Exp, bias=k.a_s[:, i:i + 1])
                    nc.scalar.activation(exp_v[:, e, 0:n * P], k.ps[:, ROWS_V, 0:n * P], ACT.Exp,
                                         bias=k.a_s5[:, i:i + 1]).then_inc(s.exp_ready, 1)
                act.wait_ge(s.out_ready, ch + 1)
                nc.scalar.activation(out_sb[0:C + 1, 0:n * P], k.ps[0:C + 1, OUT, 0:n * P], ACT.Copy).then_inc(s.out_copied, 1)

            exponentials(0, True, CHUNK)
            with act.Fori(0, NC - 1) as r:
                exponentials(r + 1, False, CHUNK)
            exponentials(NC, False, REST)

        def exact_tensor(pe):
            def turn_maxima(ch, first, n):
                pe.wait_ge(s.max_ready, ch + 1)
                if not first:
                    pe.wait_ge(s.h_written, ch - 1)
                for b in range(n):
                    last = nc.tensor.transpose(k.ps[:, TURN, b * P:(b + 1) * P], odd[:, b * P:(b + 1) * P], k.ident[:, :])
                last.then_inc(s.max_turned, 1)

            def rows(ch, first, n):
                pe.wait_ge(s.diag_ready, ch * 2 + 2)
                if not first:
                    pe.wait_ge(s.exp_ready, ch * NT)
                nc.tensor.matmul(k.ps[:, ROWS_U, 0:n * P], k.ones[:, :], diag[:, 0, 0:n * P], start=True, stop=True)
                nc.tensor.matmul(k.ps[:, ROWS_V, 0:n * P], k.ones[:, :], diag[:, 1, 0:n * P], start=True,
                                 stop=True).then_inc(s.rows_ready, 1)

            def turn_output(ch, n):
                pe.wait_ge(s.out_copied, ch + 1)
                for b in range(n):
                    last = nc.tensor.transpose(k.ps[:, TURN, b * (C + 1):(b + 1) * (C + 1)],
                                               out_sb[0:C + 1, b * P:(b + 1) * P], k.ident[0:C + 1, 0:C + 1])
                last.then_inc(s.out_turned, 1)

            def products(ch, n):
                for i in range(NT):
                    pe.wait_ge(s.prob_ready, ch * NT + (i + 1))
                    nc.tensor.matmul(k.ps[0:C + 1, OUT, 0:n * P], k.Hg[:, i, 0:C + 1], prob[:, i % 2, 0:n * P],
                                     start=i == 0, stop=i == NT - 1).then_inc(s.used, 1)
                pe.wait_ge(s.used, (ch + 1) * NT)
                pe.sem_inc(s.out_ready, 1)

            turn_maxima(0, True, CHUNK)
            rows(0, True, CHUNK)
            products(0, CHUNK)
            turn_maxima(1, True, CHUNK)
            rows(1, False, CHUNK)
            turn_output(0, CHUNK)
            products(1, CHUNK)
            with pe.Fori(0, NC - 2) as r:
                turn_maxima(r + 2, False, CHUNK)
                rows(r + 2, False, CHUNK)
                turn_output(r + 1, CHUNK)
                products(r + 2, CHUNK)
            turn_maxima(NC, False, REST)
            rows(NC, False, REST)
            turn_output(NC - 1, CHUNK)
            products(NC, REST)
            pe.wait_ge(s.h_written, NC)
            turn_output(NC, REST)

        banks = (3, 4, 5, 7)
        outs = (OUT, OTHER_OUT)

        def slot_free(eng, sem, ch, i, first):
            last = max((j for j in range(i) if RING4[j] == RING4[i]), default=None)
            if last is not None:
                eng.wait_ge(sem, ch * NT + (last + 1))
            elif not first:
                last = max(j for j in range(NT) if RING4[j] == RING4[i])
                eng.wait_ge(sem, ch * NT + (last + 1 - NT))

        def chunks(eng, body):
            body(0, 0, CHUNK, 0)
            body(1, 1, CHUNK, 1)
            with eng.Fori(1, NC // 2) as r:
                body(r * 2, 2, CHUNK, 0)
                body(r * 2 + 1, 2, CHUNK, 1)
            body(NC, 2, REST, 0)

        def small_vector(dve):
            dve.tensor_scalar(k.s1[:, :], k.a_s[:, :], 1 - SLOPE, None, ALU.mult).then_inc(t.factor, 1)
            dve.wait_ge(t.factor, 2)
            dve.tensor_tensor(k.Hg[:, :, 0:C + 1], k.Hg[:, :, 0:C + 1], k.s2[:, :].unsqueeze(2).to_broadcast([P, NT, C + 1]),
                              ALU.mult).then_inc(t.hg_ready, 1)

            def write(ch, n):
                dve.wait_ge(t.out_turned, ch + 1)
                sums = k.ps[:, TURN, 0:n * (C + 1)].rearrange("p (b q) -> p b q", q=C + 1)
                dve.reciprocal(rz[:, 0:n], sums[:, :, C]).then_inc(t.norm_ready, 1)
                dve.wait_ge(t.norm_ready, ch + 1)
                dve.tensor_tensor(k.H[:, nodes(ch, n), :], sums[:, :, 0:C], rz[:, 0:n].unsqueeze(2).to_broadcast([P, n, C]),
                                  ALU.mult).then_inc(t.h_written, 1)

            def probabilities(ch, number, n, out):
                for i in range(NT):
                    dve.wait_ge(t.exp_ready, ch * NT + (i + 1))
                    slot_free(dve, t.used, ch, i, number == 0)
                    nc.vector.scalar_tensor_tensor(out=ring[:, RING4[i], 0:n * P], in0=k.ps[:, banks[RING4[i]], 0:n * P], scalar=1.0,
                                                   in1=k.ADJ[:, i, cols(ch, n)], op0=ALU.max,
                                                   op1=ALU.mult).then_inc(t.prob_ready, 1)
                    if i == 16 and number > 0:
                        write(ch - 1, CHUNK)

            chunks(dve, probabilities)
            write(NC, REST)
            dve.wait_ge(t.h_written, NC + 1)

        def small_gpsimd(pool):
            def diagonal(ch, number, n, out):
                if number > 0:
                    pool.wait_ge(t.rows_ready, ch)
                pool.tensor_tensor(diag[:, 0, 0:n * P].rearrange("p (b q) -> p b q", q=P),
                                   k.ident[:, :].unsqueeze(1).to_broadcast([P, n, P]),
                                   k.a_d[:, nodes(ch, n)].unsqueeze(2).to_broadcast([P, n, P]), ALU.mult).then_inc(t.diag_ready, 1)

            chunks(pool, diagonal)

        def small_scalar(act):
            nc.scalar.activation(k.s2[:, :], k.a_s[:, :], ACT.Exp, scale=SLOPE).then_inc(t.factor, 1)
            act.wait_ge(t.factor, 2)

            def copy_out(ch, number, n, out):
                act.wait_ge(t.used, ch * NT + NT)
                if number > 0:
                    act.wait_ge(t.out_turned, ch)
                nc.scalar.activation(out_sb[0:C + 1, 0:n * P], k.ps[0:C + 1, outs[out], 0:n * P], ACT.Copy).then_inc(t.out_copied, 1)

            def exponentials(ch, number, n, out):
                act.wait_ge(t.rows_ready, ch + 1)
                for i in range(NT):
                    slot_free(act, t.prob_ready, ch, i, number == 0)
                    nc.scalar.activation(k.ps[:, banks[RING4[i]], 0:n * P], k.ps[:, ROWS_U, 0:n * P], ACT.Exp,
                                         bias=k.s1[:, i:i + 1], scale=1 - SLOPE).then_inc(t.exp_ready, 1)
                    if i == 6 and number > 0:
                        copy_out(ch - 1, number - 1, CHUNK, 1 - out)

            chunks(act, exponentials)
            copy_out(NC, 2, REST, 0)

        def small_tensor(pe):
            def rows(ch, first, n):
                pe.wait_ge(t.diag_ready, ch + 1)
                if not first:
                    pe.wait_ge(t.exp_ready, ch * NT)
                nc.tensor.matmul(k.ps[:, ROWS_U, 0:n * P], k.ones[:, :], diag[:, 0, 0:n * P], start=True,
                                 stop=True).then_inc(t.rows_ready, 1)

            def turn_output(ch, number, n):
                pe.wait_ge(t.out_copied, ch + 1)
                if number > 0:
                    pe.wait_ge(t.h_written, ch)
                for b in range(n):
                    last = nc.tensor.transpose(k.ps[:, TURN, b * (C + 1):(b + 1) * (C + 1)],
                                               out_sb[0:C + 1, b * P:(b + 1) * P], k.ident[0:C + 1, 0:C + 1])
                last.then_inc(t.out_turned, 1)

            def products(ch, number, n, out, following=CHUNK):
                if number > 1:
                    pe.wait_ge(t.out_copied, ch - 1)
                for i in range(NT):
                    if i == NT - 4 and following:
                        rows(ch + 1, False, following)
                    pe.wait_ge(t.prob_ready, ch * NT + (i + 1))
                    nc.tensor.matmul(k.ps[0:C + 1, outs[out], 0:n * P], k.Hg[:, i, 0:C + 1], ring[:, RING4[i], 0:n * P],
                                     start=i == 0, stop=i == NT - 1).then_inc(t.used, 1)
                    if i == 10 and number > 0:
                        turn_output(ch - 1, number - 1, CHUNK)

            rows(0, True, CHUNK)
            pe.wait_ge(t.hg_ready, 1)
            products(0, 0, CHUNK, 0)
            products(1, 1, CHUNK, 1)
            with pe.Fori(1, NC // 2 - 1) as r:
                products(r * 2, 2, CHUNK, 0)
                products(r * 2 + 1, 2, CHUNK, 1)
            products(NC - 2, 2, CHUNK, 0)
            products(NC - 1, 2, CHUNK, 1, REST)
            products(NC, 2, REST, 0, 0)
            turn_output(NC, 2, REST)

        @block.vector
        def _(dve):
            wide = dve.value_load(k.wide[0:1, 0:1], min_val=0, max_val=1)
            with dve.If(wide):
                exact_vector(dve)
            with dve.Else():
                small_vector(dve)

        @block.gpsimd
        def _(pool):
            wide = pool.value_load(k.wide[0:1, 0:1], min_val=0, max_val=1)
            with pool.If(wide):
                exact_gpsimd(pool)
            with pool.Else():
                small_gpsimd(pool)

        @block.scalar
        def _(act):
            wide = act.value_load(k.wide[0:1, 0:1], min_val=0, max_val=1)
            act.preload_act_table(ACT.Exp)
            with act.If(wide):
                exact_scalar(act)
            with act.Else():
                small_scalar(act)

        @block.tensor
        def _(pe):
            wide = pe.value_load(k.wide[0:1, 0:1], min_val=0, max_val=1)
            with pe.If(wide):
                exact_tensor(pe)
            with pe.Else():
                small_tensor(pe)


def graph_norm(nc, k, d, name, b, last):
    with ExitStack() as c:
        s = semaphores(nc, k, name, "chain vectors h_ready sums_ready centred_h squared_h squares_ready var_h dev_h "
                       "first second third fourth fifth centred squared read variance deviation normal back shifted")
        bias, weight, beta, mscale, mean, scale, dev = (
            c.enter_context(nc.sbuf_tensor(f"{name}_{n}", [P, C], F32)) for n in "bias weight beta mscale mean scale dev".split())
        if last:
            R = c.enter_context(nc.sbuf_tensor(f"{name}_R", [P, NT, C], F32))
        block = c.enter_context(nc.Block())
        sums, squares = k.ps[:, 5, 0:C], k.ps[:, 6, 0:C]

        @block.sync
        def _(sp):
            load_rows(sp, [(bias, b), (weight, d.gn_weight), (beta, d.gn_bias), (mscale, d.gn_mean_scale)], s.vectors)
            if last:
                sp.dma_start(R[:, :, :], d.residual).then_inc(s.back, 16)
                sp.wait_ge(s.back, 16)
            sp.wait_ge(s.vectors, 4 * 16)

        if last:
            @block.gpsimd
            def _(pool):
                adj = flat(k.ADJ[:, :, :])
                most = adj[:, 0:(NT - 1) * (NP + P)].rearrange("p (t q) -> p t q", q=NP + P)[:, :, 0:P]
                pool.tensor_tensor(most, most, k.ident_h[:, :].unsqueeze(1).to_broadcast([P, NT - 1, P]),
                                   ALU.subtract)
                end = adj[:, (NT - 1) * (NP + P):NT * NP]
                pool.tensor_tensor(end, end, k.ident_h[:, :], ALU.subtract)
                pool.wait_ge(s.back, 16)
                pool.wait_ge(s.vectors, 4 * 16)
                pool.tensor_tensor(R[:, :, :], R[:, :, :], down(beta[:, :]), ALU.add).then_inc(s.shifted, 1)

        @block.vector
        def _(dve):
            chain = Chain(dve, s.chain)
            dve.wait_ge(s.vectors, 4 * 16)
            for g in range(NG):
                dve.tensor_tensor(tiles(k.H, g), tiles(k.H, g), down(bias[:, :], G), ALU.add).then_inc(s.h_ready, 1)
            dve.wait_ge(s.sums_ready, 1)
            chain(nc.vector.scalar_tensor_tensor(out=mean[:, :], in0=sums, scalar=1.0 / N, in1=mscale[:, :],
                                                 op0=ALU.mult, op1=ALU.mult))
            for g in range(NG):
                dve.tensor_tensor(tiles(k.H, g), tiles(k.H, g), down(mean[:, :], G), ALU.subtract).then_inc(s.centred_h, 1)
            dve.wait_ge(s.squares_ready, 1)
            dve.tensor_scalar(scale[:, :], squares, 1.0 / N, GN_EPS, ALU.mult, ALU.add).then_inc(s.var_h, 1)
            dve.wait_ge(s.dev_h, 1)
            chain(dve.reciprocal(scale[:, :], dev[:, :]))
            chain(dve.tensor_tensor(scale[:, :], scale[:, :], weight[:, :], ALU.mult))
            if last:
                dve.wait_ge(s.shifted, 1)

            def step(n, g):
                H = tiles(k.H, g)
                if n == 0:
                    dve.tensor_tensor(H, H, down(scale[:, :], G), ALU.mult).then_inc(s.first, 1)
                elif n == 1:
                    dve.wait_ge(s.first, g + 1)
                    dve.tensor_tensor(H, H, tiles(R, g) if last else down(beta[:, :], G), ALU.add).then_inc(s.second, 1)
                elif n == 2:
                    dve.wait_ge(s.second, g + 1)
                    nc.vector.scalar_tensor_tensor(out=H, in0=H, scalar=0.01, in1=H, op0=ALU.mult, op1=ALU.max).then_inc(s.third, 1)
                elif n == 3:
                    dve.wait_ge(s.third, g + 1)
                    dve.tensor_tensor(tiles(k.X, g), tiles(k.X, g), H, ALU.add).then_inc(s.fourth, 1)
                elif n == 4:
                    dve.wait_ge(s.fourth, g + 1)
                    dve.tensor_reduce(group(k.s1, g), tiles(k.X, g), axis=AX, op=ALU.add).then_inc(s.fifth, 1)

            steps = 5 if last else 3
            for q in range(NG + steps - 1):
                for n in range(steps):
                    if 0 <= q - n < NG:
                        step(n, q - n)
            if last:
                dve.wait_ge(s.fifth, NG)
                chain(dve.tensor_scalar(k.s1[:, :], k.s1[:, :], 1.0 / C, None, ALU.mult))
                for g in range(NG):
                    dve.tensor_tensor(tiles(k.H, g), tiles(k.X, g), across(group(k.s1, g)), ALU.subtract).then_inc(s.centred, 1)
                    if g >= 1:
                        dve_square_sum(k, dve, g - 1, s.squared, s.read)
                dve_square_sum(k, dve, NG - 1, s.squared, s.read)
                dve_normalise(nc, k, dve, chain, s.read, s.variance, s.deviation, s.normal)

        @block.scalar
        def _(act):
            for g in range(NG):
                act.wait_ge(s.centred_h, g + 1)
                nc.scalar.activation(tiles(k.T, g), tiles(k.H, g), ACT.Square).then_inc(s.squared_h, 1)
            act.wait_ge(s.var_h, 1)
            nc.scalar.activation(dev[:, :], scale[:, :], ACT.Sqrt).then_inc(s.dev_h, 1)
            if last:
                for g in range(NG):
                    act_square(nc, k, act, g, s.centred, s.squared, s.read)
                act_deviation(nc, k, act, s.variance, s.deviation)

        @block.tensor
        def _(pe):
            for g in range(NG):
                last_sum = pe_column_sums(nc, k, pe, s.h_ready, k.H, sums, g)
            last_sum.then_inc(s.sums_ready, 1)
            for g in range(NG):
                last_sum = pe_column_sums(nc, k, pe, s.squared_h, k.T, squares, g)
            last_sum.then_inc(s.squares_ready, 1)


BATCH = 5
NBATCH = NT // BATCH
BEHIND = 2


def sum_over_sources(nc, k, d):
    with ExitStack() as c:
        s = semaphores(nc, k, "l3", "chain value high y_ready turned copied_v copied_a used emptied final stored")
        back = c.enter_context(nc.sbuf_tensor("l3_back", [P, NBATCH, BATCH * P], F16))
        block = c.enter_context(nc.Block())
        bank = [k.ps[:, b, 0:BATCH * P // 2].bitcast(F16) for b in range(NBATCH)]
        share = {0: (NBATCH + 1) // 2, 1: NBATCH // 2}

        def copied(eng, j, m):
            eng.wait_ge(s.copied_v if m % 2 else s.copied_a, j * share[m % 2] + (m // 2 + 1))

        def may_copy(eng, j, m):
            eng.wait_ge(s.turned, j * NBATCH + (m + 1))
            if j:
                eng.wait_ge(s.used, j * NBATCH + (m + 1 - NBATCH))

        @block.vector
        def _(dve):
            chain = Chain(dve, s.chain)
            for g in range(NG):
                dve.tensor_tensor(tiles(k.H, g), tiles(k.H, g), across(group(k.dis, g)), ALU.mult).then_inc(s.value, 1)
                if g >= 1:
                    dve_low(nc, k, dve, g - 1, s.high, s.y_ready)
            dve_low(nc, k, dve, NG - 1, s.high, s.y_ready)

            def copies(j):
                for m in range(1, NBATCH, 2):
                    may_copy(dve, j, m)
                    dve.tensor_copy(back[:, m, :], bank[m]).then_inc(s.copied_v, 1)

            def collect(j):
                dve.wait_ge(s.used, (j + 1) * NBATCH)
                add_parts(nc, k, tiles(k.H, j, 1), 5 + j % 3).then_inc(s.emptied, 1)
                if j % G == G - 1:
                    g = j // G
                    dve.wait_ge(s.emptied, j + 1)
                    chain(unscaled(nc, k, k.dis, g))
                    dve.tensor_tensor(tiles(k.X, g), tiles(k.X, g), tiles(k.H, g), ALU.add).then_inc(s.final, 1)

            dve.wait_ge(s.y_ready, NG)
            copies(0)
            for j in range(NT):
                if j + 1 < NT:
                    copies(j + 1)
                collect(j)

        @block.scalar
        def _(act):
            for g in range(NG):
                act.wait_ge(s.value, g + 1)
                act_high(nc, k, g, s.high)
            for j in range(NT):
                for m in range(0, NBATCH, 2):
                    may_copy(act, j, m)
                    nc.scalar.activation(back[:, m, :], bank[m], ACT.Copy).then_inc(s.copied_a, 1)

        @block.tensor
        def _(pe):
            def turn(j, m):
                if j:
                    copied(pe, j - 1, m)
                for i in range(BATCH):
                    last = nc.tensor.transpose(bank[m][:, i * P:(i + 1) * P],
                                               k.ADJ[:, j, (m * BATCH + i) * P:(m * BATCH + i + 1) * P], k.ident_h[:, :])
                last.then_inc(s.turned, 1)

            def use(j, m):
                copied(pe, j, m)
                if j == 0:
                    pe.wait_ge(s.y_ready, m + 1)
                if m == 0 and j >= 3:
                    pe.wait_ge(s.emptied, j - 2)
                for i in range(BATCH):
                    last = nc.tensor.matmul(k.ps[:, 5 + j % 3, 0:ONE], back[:, m, i * P:(i + 1) * P], k.Y[:, m * BATCH + i, 0:ONE],
                                            start=m == 0 and i == 0, stop=m == NBATCH - 1 and i == BATCH - 1)
                last.then_inc(s.used, 1)

            for q in range(NT * NBATCH + BEHIND):
                if q < NT * NBATCH:
                    turn(*divmod(q, NBATCH))
                if q >= BEHIND:
                    use(*divmod(q - BEHIND, NBATCH))

        @block.sync
        def _(sp):
            for g in range(NG):
                sp.wait_ge(s.final, g + 1)
                if g < NG - 1:
                    sp.dma_start(d.out[g * G * P:(g + 1) * G * P, :].rearrange("(t p) f -> p t f", p=P),
                                 tiles(k.X, g)).then_inc(s.stored, 16)
            sp.dma_start(d.out[(NG - 1) * G * P:(NT - 1) * P, :].rearrange("(t p) f -> p t f", p=P),
                         k.X[:, (NG - 1) * G:NT - 1, :]).then_inc(s.stored, 16)
            sp.dma_start(d.out[(NT - 1) * P:N, :], k.X[0:LAST, NT - 1, :]).then_inc(s.stored, 16)
            sp.wait_ge(s.stored, (NG + 1) * 16)


class OnChip:
    pass


def network(nc, d):
    with ExitStack() as c:
        def sb(name, shape, dt):
            return c.enter_context(nc.sbuf_tensor(name, shape, dt))

        k = OnChip()
        k.held = []
        k.ADJ = sb("adjacency", [P, NT, NP], F16)
        k.X = sb("x_sb", [P, NT, C], F32)
        k.ident, k.ident_h = sb("ident", [P, P], F32), sb("ident_h", [P, P], F16)
        k.ones, k.ones_h = sb("ones", [P, P], F32), sb("ones_h", [P, 2], F16)
        k.out_deg = sb("out_deg", [P, NT], F32)
        with ExitStack() as c2:
            k.start_i = c2.enter_context(nc.sbuf_tensor("start_i", [1, NW], I32))
            locate_and_load(nc, k, d)
            build_adjacency(nc, k, d)
        k.H = sb("h_sb", [P, NT, C], F32)
        y32 = sb("y_sb", [P, 3625], F32)[:, :]
        k.Y = y32[:, 0:NT * YC // 2].bitcast(F16).rearrange("p (t f) -> p t f", f=YC)
        k.T = y32[:, 0:NT * C].rearrange("p (t f) -> p t f", f=C)
        k.Hg = y32[:, 0:NT * (C + 2)].rearrange("p (t f) -> p t f", f=C + 2)
        k.spare = y32[:, NT * (C + 2):]
        k.T2 = y32[:, NT * YC // 2:NT * YC // 2 + 2 * G * C].rearrange("p (a t f) -> p a t f", a=2, f=C)
        k.s1, k.s2, k.s3, k.out_norm, k.in_norm, k.in_deg, k.inv_deg, k.dis, k.a_s, k.a_s5, k.a_unit, k.a_d = (
            sb(n, [P, NT], F32) for n in "s1 s2 s3 out_norm in_norm in_deg inv_deg dis a_s a_s5 a_unit a_d".split())
        k.unscale = sb("unscale", [P, 2], F32)
        k.wide = sb("wide", [1, 1], I32)
        k.ps = c.enter_context(nc.psum_tensor("banks", [P, 8, 512], F32))
        convolutions(nc, k, d)
        sage(nc, k, d)
        prepare_attention(nc, k, d, "prep1", d.W1, d.att_src1, d.att_dst1, True)
        attend(nc, k, d, "gat1")
        clear_semaphores(nc, k)
        graph_norm(nc, k, d, "norm1", d.gat_b1, False)
        prepare_attention(nc, k, d, "prep2", d.W2, d.att_src2, d.att_dst2, False)
        attend(nc, k, d, "gat2")
        graph_norm(nc, k, d, "norm2", d.gat_b2, True)
        sum_over_sources(nc, k, d)


INPUTS = {
    "x": "x", "src": "src", "dst": "dst",
    "L0_gnn_bias1": "bias1", "L0_gnn_bias2": "bias2", "L0_gnn_gamma": "gamma", "L0_gnn_beta": "beta",
    "L1_gnn_W_self1": "W_self1", "L1_gnn_W_neigh1": "W_neigh1", "L1_gnn_b1": "b1",
    "L1_gnn_W_self2": "W_self2", "L1_gnn_W_neigh2": "W_neigh2", "L1_gnn_b2": "b2",
    "L2_gnn_W1": "W1", "L2_gnn_att_src1": "att_src1", "L2_gnn_att_dst1": "att_dst1", "L2_gnn_b1": "gat_b1",
    "L2_gnn_W2": "W2", "L2_gnn_att_src2": "att_src2", "L2_gnn_att_dst2": "att_dst2", "L2_gnn_b2": "gat_b2",
    "L2_gnn_gn_weight": "gn_weight", "L2_gnn_gn_bias": "gn_bias", "L2_gnn_gn_mean_scale": "gn_mean_scale",
}


def program(nc, shapes):
    arrays = {short: nc.dram_tensor(f"in_{name}", shapes[name][0], shapes[name][1], kind="ExternalInput").ap()
              for name, short in INPUTS.items()}
    arrays["keys"] = nc.dram_tensor("edge_keys", [E], I32).ap()
    arrays["residual"] = nc.dram_tensor("residual", [P, NT, C], F32).ap()
    arrays["out"] = nc.dram_tensor("out_x", [N, C], F32, kind="ExternalOutput").ap()
    d = namedtuple("Dram", list(arrays))(*arrays.values())
    network(nc, d)


def kernel(**inputs):
    import numpy as np
    import concourse.bacc as bacc
    from concourse.bass_utils import run_bass_kernel_spmd

    nc = bacc.Bacc("TRN2", target_bir_lowering=False, num_devices=1)
    arrays = {f"in_{name}": np.ascontiguousarray(inputs[name]) for name in INPUTS}
    program(nc, {name: (arrays[f"in_{name}"].shape, mybir.dt.from_np(arrays[f"in_{name}"].dtype)) for name in INPUTS})
    r = run_bass_kernel_spmd(nc, [arrays], core_ids=[0])
    return r.results[0]["out_x"]
```

```python
from collections import namedtuple
from contextlib import ExitStack, contextmanager

import concourse.bass as bass
from concourse import mybir

F32, F16 = mybir.dt.float32, mybir.dt.float16
I32 = mybir.dt.int32
ALU = mybir.AluOpType
ACT = mybir.ActivationFunctionType
AX = mybir.AxisListType.X

P = 128
N = 3125
E = 100000
C = 96
NT = -(-N // P)
NP = NT * P
LAST = N - (NT - 1) * P
G = 5
NG = NT // G

EP, EF = 125, E // 125
SRC_BITS = 12
W = 16
NW = -(-N // W)
WT = 5
PAIR = 2 * WT
WE = WT * P
STEP = 25
NS = EF // STEP
CODES = NT * W
BASE = 1024
RING = 4
LOADS = 7
LW = NW // LOADS
LOADS_AT_ONCE = 7
STORE_BEHIND = 3
UNIT = 0.25
LN_EPS = 1e-5


class Chain:

    def __init__(self, eng, sem):
        self.eng, self.sem, self.n, self.reg, self.per = eng, sem, 0, None, 0

    def value(self):
        return self.n if self.reg is None else self.reg * self.per + self.n

    def __call__(self, ins):
        ins.then_inc(self.sem, 1)
        self.n += 1
        self.eng.wait_ge(self.sem, self.value())

    def lag(self, ins):
        ins.then_inc(self.sem, 1)
        self.n += 1
        self.eng.wait_ge(self.sem, self.value() - 1)

    def later(self, ins):
        ins.then_inc(self.sem, 1)
        self.n += 1

    def all(self):
        self.eng.wait_ge(self.sem, self.value())

    def loop(self, reg, per):
        self.reg, self.per, self.n0 = reg, per, self.n

    def end(self, trips):
        assert self.n - self.n0 == self.per, (self.n, self.n0, self.per)
        self.reg, self.n = None, self.n0 + trips * self.per


def semaphores(nc, k, phase, names):
    held = namedtuple(phase, names)(*[nc.alloc_semaphore(f"{phase}_{n}") for n in names.split()])
    k.held.extend(held)
    return held


def clear_semaphores(nc, k):
    nc.clear_and_free_semaphores(k.held)
    nc.all_engine_barrier()
    k.held = []


@contextmanager
def phases(nc):
    with ExitStack() as c:
        with ExitStack() as inner:
            yield c, inner.enter_context(nc.Block())


def flat(ap):
    return ap.rearrange("p a b -> p (a b)")


def locate_and_load(nc, k, d):
    with ExitStack() as c:
        def sb(name, shape, dt):
            return c.enter_context(nc.sbuf_tensor(name, shape, dt))

        def sem(name):
            return nc.alloc_semaphore(name)

        src = sb("src_i", [EP, EF], I32)
        dst = sb("dst_i", [EP, EF], I32)
        key = sb("key_i", [EP, EF], I32)
        sample = sb("sample", [EP, NS], F32)
        bound = sb("bound", [EP, NW], F32)
        below = sb("below", [EP, NS, NW], F16)
        start_f = sb("start_f", [1, NW], F32)
        count_ps = c.enter_context(nc.psum_tensor("count_ps", [1, NW], F32))
        edges_in, x_in, pads = sem("edges_in"), sem("x_in"), sem("pads")
        bounds_ready, key_ready, key_out = sem("bounds_ready"), sem("key_ready"), sem("key_out")
        below_ready, count_ready = sem("below_ready"), sem("count_ready")
        dve_chain, pool_chain = sem("dve_chain0"), sem("pool_chain0")
        block = c.enter_context(nc.Block())

        @block.sync
        def _(sp):
            sp.dma_start(dst[:, :], d.dst.rearrange("(p f) -> p f", p=EP)).then_inc(edges_in, 16)
            sp.dma_start(src[:, :], d.src.rearrange("(p f) -> p f", p=EP)).then_inc(edges_in, 16)
            sp.wait_ge(pads, 1)
            sp.dma_start(k.X[:, 0:NT - 1, :], d.x[0:(NT - 1) * P, :].rearrange("(t p) f -> p t f", p=P)).then_inc(x_in, 16)
            sp.dma_start(k.X[0:LAST, NT - 1, :], d.x[(NT - 1) * P:N, :]).then_inc(x_in, 16)
            sp.wait_ge(key_ready, 1)
            sp.dma_start(d.keys.rearrange("(p f) -> p f", p=EP), key[:, :]).then_inc(key_out, 16)
            sp.wait_ge(x_in, 32)
            sp.wait_ge(key_out, 16)

        @block.gpsimd
        def _(pool):
            pool.iota(bound[:, :], pattern=[[W, NW]], base=0, channel_multiplier=0,
                      allow_small_or_imprecise_dtypes=True).then_inc(bounds_ready, 1)
            chain = Chain(pool, pool_chain)
            chain(pool.memset(k.ident[:, :], 0.0))
            chain(pool.affine_select(out=k.ident[:, :], in_=k.ident[:, :], compare_op=ALU.not_equal, fill=1.0,
                                     base=0, pattern=[[-1, P]], channel_multiplier=1))
            chain(pool.tensor_copy(k.ident_h[:, :], k.ident[:, :]))
            chain(pool.tensor_scalar(k.loops_h[:, :], k.ident[:, :], UNIT, None, ALU.mult))

        @block.vector
        def _(dve):
            chain = Chain(dve, dve_chain)
            dve.memset(k.X[:, NT - 1, :], 0.0).then_inc(pads, 1)
            chain(dve.memset(k.ones_h[:, :], 1.0))
            chain(dve.memset(k.ones[:, :], 1.0))
            dve.wait_ge(edges_in, 32)
            nc.vector.scalar_tensor_tensor(out=key[:, :], in0=dst[:, :], scalar=float(1 << SRC_BITS), in1=src[:, :],
                                           op0=ALU.mult, op1=ALU.add).then_inc(key_ready, 1)
            chain(dve.tensor_copy(sample[:, :], dst[:, :].rearrange("p (s j) -> p s j", j=STEP)[:, :, 0]))
            dve.wait_ge(bounds_ready, 1)
            for s in range(NS):
                last = dve.tensor_scalar(below[:, s, :], bound[:, :], sample[:, s:s + 1], None, ALU.is_gt)
            last.then_inc(below_ready, 1)
            dve.wait_ge(count_ready, 1)
            chain(dve.tensor_scalar(start_f[:, :], count_ps[:, :], -1.0, 0.0, ALU.add, ALU.max))
            chain(dve.tensor_scalar(k.start_i[:, :], start_f[:, :], float(STEP), float(E - WE), ALU.mult, ALU.min))

        @block.tensor
        def _(pe):
            pe.wait_ge(below_ready, 1)
            for s in range(NS):
                last = nc.tensor.matmul(count_ps[:, :], k.ones_h[0:EP, 0:1], below[:, s, :], start=s == 0, stop=s == NS - 1)
            last.then_inc(count_ready, 1)


def build_adjacency(nc, k, d):
    with ExitStack() as c:
        def sb(name, shape, dt):
            return c.enter_context(nc.sbuf_tensor(name, shape, dt))

        def sem(name):
            return nc.alloc_semaphore(name)

        ncol = NW * WT
        lcol = LW * WT
        window_keys = sb("window_keys", [P, ncol], I32)
        low_i = sb("low_i", [P, 3, lcol], I32)
        row = sb("row", [P, ncol], F16)
        code = window_keys[:, :].bitcast(F32)
        negative = sb("negative", [P, NW], F32)
        inside = sb("inside", [P, ncol], F16)
        own = sb("own", [P, ncol], F16)
        rows_iota = sb("rows_iota", [P, P, PAIR], F16)
        codes_iota = sb("codes_iota", [P, CODES], F16)
        hot_row = sb("hot_row", [P, RING // 2, P, PAIR], F16)
        hot_code = sb("hot_code", [P, RING, WT, CODES], F16)
        distance = sb("distance", [P, RING, CODES], F16)
        zeros = sb("zeros", [P, P], F16)
        inside_sum = sb("inside_sum", [P, 1], F32)
        missed = sb("missed", [1, 1], I32)
        this_window = sb("this_window", [P, 1], F32)
        counts = c.enter_context(nc.psum_tensor("counts", [P, RING, 512], F32))
        degree_ps = c.enter_context(nc.psum_tensor("degree_ps", [P, 512], F32))
        total_ps = c.enter_context(nc.psum_tensor("total_ps", [P, 512], F32))
        window_in = [sem(f"window_in{n}") for n in range(LOADS)]
        iotas = sem("iotas")
        hot_ready, counted, stored = sem("hot_ready"), sem("counted"), sem("stored")
        codes_ready, distance_ready, act_hot_ready = sem("codes_ready"), sem("distance_ready"), sem("act_hot_ready")
        degree_ready, total_ready, flag_ready = sem("degree_ready"), sem("total_ready"), sem("flag_ready")
        g_keys_in, g_hot_ready, g_counted, g_window_done, g_stored, g_degree_ready = (
            sem("g_keys_in"), sem("g_hot_ready"), sem("g_counted"), sem("g_window_done"), sem("g_stored"), sem("g_degree_ready"))
        zeros_ready, sum_ready = sem("zeros_ready"), sem("sum_ready")
        dve_chain, pool_chain = sem("dve_chain1"), sem("pool_chain1")
        block = c.enter_context(nc.Block())
        rounds = NW // RING
        scratch_cols = 2 * C
        batches = EF // WT
        g_code, g_place, g_window = code[0:EP, 0:EF], inside[0:EP, 0:EF], own[0:EP, 0:EF]

        def load_windows(eng, load, first, rounds, at_once):
            with eng.Fori(0, rounds) as r:
                at = [eng.value_load(k.start_i[0:1, bass.ds(r * at_once + (load * LW + first + b), 1)], min_val=0, max_val=E - WE)
                      for b in range(at_once)]
                for b in range(at_once):
                    w = r * at_once + (load * LW + first + b)
                    eng.dma_start(window_keys[:, bass.ds(w * WT, WT)],
                                  d.keys[bass.ds(at[b], WE)].rearrange("(p j) -> p j", j=WT)).then_inc(window_in[load], 16)

        @block.gpsimd
        def _(pool):
            pool.iota(rows_iota[:, :, :], pattern=[[1, P], [0, PAIR]], base=0, channel_multiplier=0,
                      allow_small_or_imprecise_dtypes=True).then_inc(iotas, 1)
            pool.iota(codes_iota[:, :], pattern=[[1, CODES]], base=BASE, channel_multiplier=0,
                      allow_small_or_imprecise_dtypes=True).then_inc(iotas, 1)
            pool.iota(own[:, :], pattern=[[1, NW], [0, WT]], base=0, channel_multiplier=0,
                      allow_small_or_imprecise_dtypes=True).then_inc(iotas, 1)

        @block.vector
        def _(dve):
            chain = Chain(dve, dve_chain)
            dve.memset(zeros[:, :], 0.0).then_inc(zeros_ready, 1)
            chain(dve.memset(k.ADJ[:, :, NW * W:NP], 0.0))
            dve.sem_inc(counted, RING)
            centred = k.ADJ[:, :, NW * W - scratch_cols:NW * W].bitcast(F32)
            chain(dve.tensor_reduce(k.mean0[:, :], k.X[:, :, :], axis=AX, op=ALU.add))
            chain(dve.tensor_scalar(k.mean0[:, :], k.mean0[:, :], 1.0 / C, None, ALU.mult))
            chain(dve.tensor_tensor(centred, k.X[:, :, :], across(k.mean0[:, :]), ALU.subtract))
            chain(dve.tensor_tensor(centred, centred, centred, ALU.mult))
            chain(dve.tensor_reduce(k.var0[:, :], centred, axis=AX, op=ALU.add))
            chain(dve.tensor_scalar(k.var0[:, :], k.var0[:, :], 1.0 / C, LN_EPS, ALU.mult, ALU.add))
            dve.wait_ge(iotas, 3)
            lo, mid, row_i = (low_i[:, n, :] for n in range(3))
            for load in range(LOADS):
                at = slice(load * lcol, (load + 1) * lcol)
                keys = window_keys[:, at]
                dve.wait_ge(window_in[load], 16 * LW)
                chain.later(dve.tensor_scalar(row_i, keys, P - 1, None, ALU.bitwise_and))
                chain.later(dve.tensor_scalar(lo, keys, 3, 0x1F0, ALU.logical_shift_right, ALU.bitwise_and))
                chain(dve.tensor_scalar(mid, keys, SRC_BITS, W - 1, ALU.logical_shift_right, ALU.bitwise_and))
                chain(dve.tensor_scalar(keys, keys, SRC_BITS + 4, None, ALU.logical_shift_right))
                chain.later(dve.tensor_copy(row[:, at], row_i))
                chain(dve.tensor_tensor(inside[:, at], keys, own[:, at], ALU.is_equal))
                chain(dve.tensor_tensor(code[:, at], lo, mid, ALU.add))
                chain(nc.vector.scalar_tensor_tensor(out=code[:, at], in0=inside[:, at], scalar=float(BASE), in1=code[:, at],
                                                     op0=ALU.mult, op1=ALU.add))
                dve.tensor_scalar(negative[:, load * LW:(load + 1) * LW],
                                  code[:, at].rearrange("p (w j) -> p w j", j=WT)[:, :, WT - 1],
                                  -1.0, None, ALU.mult).then_inc(codes_ready, 1)
                with dve.Fori(0, LW // RING) as r:
                    for b in range(RING):
                        w = r * RING + (load * LW + b)
                        if b % 2 == 0:
                            dve.wait_ge(counted, w + 2)
                            dve.tensor_tensor(hot_row[:, b // 2, :, :], rows_iota[:, :, :],
                                              row[:, bass.ds(w * WT, PAIR)].unsqueeze(1).to_broadcast([P, P, PAIR]), ALU.is_equal)
                        for j in range(WT - 1):
                            col = bass.ds(w * WT + j, 1)
                            last = dve.tensor_scalar(hot_code[:, b, j, :], codes_iota[:, :], code[:, col], None, ALU.is_equal)
                        last.then_inc(hot_ready, 1)
            dve.tensor_reduce(inside_sum[:, :], inside[:, :], axis=AX, op=ALU.add).then_inc(sum_ready, 1)
            dve.wait_ge(degree_ready, 1)
            chain(dve.tensor_reduce(k.out_deg[:, :], degree_ps[:, 0:CODES].rearrange("p (t w) -> p t w", w=W), axis=AX, op=ALU.add))
            chain(dve.tensor_scalar(k.out_deg[:, :], k.out_deg[:, :], 1 / UNIT, None, ALU.mult))
            dve.wait_ge(total_ready, 1)
            dve.tensor_scalar(missed[:, :], total_ps[0:1, 0:1], float(E), None, ALU.is_lt).then_inc(flag_ready, 1)
            dve.wait_ge(flag_ready, 1)
            again = dve.value_load(missed[0:1, 0:1], min_val=0, max_val=1)
            with dve.If(again):
                dve.sem_inc(g_counted, RING)
                dve.wait_ge(g_keys_in, 16)
                for at in range(0, EF, lcol):
                    n = min(lcol, EF - at)
                    keys, lo, mid = window_keys[0:EP, at:at + n], low_i[0:EP, 0, 0:n], low_i[0:EP, 1, 0:n]
                    chain(dve.tensor_scalar(lo, keys, P - 1, None, ALU.bitwise_and))
                    chain(dve.tensor_copy(row[0:EP, at:at + n], lo))
                    chain(dve.tensor_scalar(lo, keys, 3, 0x1F0, ALU.logical_shift_right, ALU.bitwise_and))
                    chain(dve.tensor_scalar(mid, keys, SRC_BITS, W - 1, ALU.logical_shift_right, ALU.bitwise_and))
                    chain(dve.tensor_tensor(g_place[:, at:at + n], lo, mid, ALU.add))
                    chain(dve.tensor_scalar(lo, keys, SRC_BITS + 4, None, ALU.logical_shift_right))
                    chain(dve.tensor_copy(g_window[:, at:at + n], lo))
                chain(dve.memset(this_window[:, :], 0.0))
                with dve.Fori(0, NW) as w:
                    chain.loop(w, 3)
                    dve.wait_ge(g_counted, w * batches + RING)
                    chain.all()
                    chain(dve.tensor_scalar(g_code, g_window, this_window[0:EP, :], float(BASE), ALU.is_equal, ALU.mult))
                    chain(dve.tensor_tensor(g_code, g_code, g_place, ALU.add))
                    chain.later(dve.tensor_scalar(this_window[:, :], this_window[:, :], 1.0, None, ALU.add))
                    with dve.Fori(0, batches // RING) as r:
                        for b in range(RING):
                            if b % 2 == 0:
                                dve.wait_ge(g_counted, w * batches + r * RING + (b + 2))
                                dve.tensor_tensor(hot_row[0:EP, b // 2, :, :], rows_iota[0:EP, :, :],
                                                  row[0:EP, bass.ds(r * RING * WT + b * WT, PAIR)].unsqueeze(1)
                                                  .to_broadcast([EP, P, PAIR]),
                                                  ALU.is_equal)
                            for j in range(WT):
                                last = dve.tensor_scalar(hot_code[0:EP, b, j, :], codes_iota[0:EP, :],
                                                         code[0:EP, bass.ds(r * RING * WT + (b * WT + j), 1)], None, ALU.is_equal)
                            last.then_inc(g_hot_ready, 1)
                chain.end(NW)
                dve.wait_ge(g_degree_ready, 1)
                chain(dve.tensor_reduce(k.out_deg[:, :], degree_ps[:, 0:CODES].rearrange("p (t w) -> p t w", w=W), axis=AX,
                                        op=ALU.add))
                chain(dve.tensor_scalar(k.out_deg[:, :], k.out_deg[:, :], 1 / UNIT, None, ALU.mult))

        @block.tensor
        def _(pe):
            pe.wait_ge(zeros_ready, 1)
            pe.wait_ge(iotas, 3)

            def window(w, b):
                pe.wait_ge(hot_ready, w + 1)
                pe.wait_ge(act_hot_ready, w + 1)
                pe.wait_ge(stored, w + 1)
                for j in range(WT):
                    last = nc.tensor.matmul(counts[:, b, 0:CODES], hot_row[:, b // 2, :, b % 2 * WT + j], hot_code[:, b, j, :],
                                            start=j == 0, stop=j == WT - 1)
                last.then_inc(counted, 1)

            def degree(w, stop=False):
                pe.wait_ge(stored, RING + 1 + w)
                return nc.tensor.matmul(degree_ps[:, 0:CODES], k.ident_h[:, :],
                                        k.ADJ[:, :, bass.ds(w * W, W)], start=False, stop=stop)

            nc.tensor.matmul(degree_ps[:, 0:CODES], zeros[:, :],
                             flat(rows_iota[:, :, :])[:, 0:CODES], start=True, stop=False)
            for b in range(RING):
                window(b, b)
            with pe.Fori(1, rounds) as r:
                for b in range(RING):
                    degree(r * RING + (b - RING))
                    window(r * RING + b, b)
            for b in range(RING):
                last = degree(NW - RING + b, stop=b == RING - 1)
            last.then_inc(degree_ready, 1)
            pe.wait_ge(sum_ready, 1)
            nc.tensor.matmul(total_ps[0:1, 0:1], inside_sum[:, :], k.ones[:, 0:1], start=True, stop=True).then_inc(total_ready, 1)
            pe.wait_ge(flag_ready, 1)
            again = pe.value_load(missed[0:1, 0:1], min_val=0, max_val=1)
            with pe.If(again):
                def clear(out, stop=False):
                    return nc.tensor.matmul(out, zeros[:, :], flat(rows_iota[:, :, :])[:, 0:CODES], start=not stop, stop=stop)

                clear(degree_ps[:, 0:CODES])
                with pe.Fori(0, NW) as w:
                    pe.wait_ge(g_stored, w + 1)
                    clear(counts[:, 0, 0:CODES])
                    with pe.Fori(0, batches // RING) as r:
                        for b in range(RING):
                            pe.wait_ge(g_hot_ready, w * batches + r * RING + (b + 1))
                            for j in range(WT):
                                last = nc.tensor.matmul(counts[:, 0, 0:CODES], hot_row[0:EP, b // 2, :, b % 2 * WT + j],
                                                        hot_code[0:EP, b, j, :], start=False, stop=False)
                            last.then_inc(g_counted, 1)
                    clear(counts[:, 0, 0:CODES], stop=True).then_inc(g_window_done, 1)
                    pe.wait_ge(g_stored, w + 2)
                    nc.tensor.matmul(degree_ps[:, 0:CODES], k.ident_h[:, :], k.ADJ[:, :, bass.ds(w * W, W)], start=False,
                                     stop=False)
                clear(degree_ps[:, 0:CODES], stop=True).then_inc(g_degree_ready, 1)

        @block.scalar
        def _(act):
            act.preload_act_table(ACT.Copy)
            act.sem_inc(stored, RING)
            load_windows(act, 0, LW // 2, LW // 2 // LOADS_AT_ONCE, LOADS_AT_ONCE)

            def distances(w, b, first=False):
                if not first:
                    act.wait_ge(act_hot_ready, w - 2 - b % 2)
                nc.scalar.activation(distance[:, b, :], codes_iota[:, :], ACT.Abs,
                                     bias=negative[:, bass.ds(w, 1)]).then_inc(distance_ready, 1)

            def one_hot(w, b):
                act.wait_ge(counted, w + 1)
                act.wait_ge(distance_ready, w + 1)
                nc.scalar.activation(hot_code[:, b - 1:b + 1, WT - 1, :], distance[:, b - 1:b + 1, :], ACT.Relu, scale=-1.0,
                                     bias=1.0).then_inc(act_hot_ready, 2)

            def store(w, b):
                act.wait_ge(counted, RING + 2 + w)
                nc.scalar.activation(k.ADJ[:, :, bass.ds(w * W, 2 * W)].rearrange("p t (b w) -> p b t w", w=W),
                                     counts[:, b:b + 2, 0:CODES].rearrange("p b (t w) -> p b t w", w=W),
                                     ACT.Copy, scale=UNIT).then_inc(stored, 2)

            act.wait_ge(iotas, 3)
            for load in range(LOADS):
                act.wait_ge(codes_ready, load + 1)
                if load == 0:
                    for b in range(RING):
                        distances(b, b, first=True)
                        if b == STORE_BEHIND:
                            store(0, 0)
                        if b % 2 == 1:
                            one_hot(b, b)
                with act.Fori(1 if load == 0 else 0, LW // RING) as r:
                    for b in range(RING):
                        w = r * RING + (load * LW + b)
                        distances(w, b)
                        if b % 2 == 1:
                            one_hot(w, b)
                            store(r * RING + (load * LW + b - STORE_BEHIND), (b - STORE_BEHIND) % RING)
            store(NW - 2, RING - 2)
            act.wait_ge(stored, RING + NW)
            act.wait_ge(flag_ready, 1)
            again = act.value_load(missed[0:1, 0:1], min_val=0, max_val=1)
            with act.If(again):
                act.sem_inc(g_stored, 1)
                with act.Fori(0, NW) as w:
                    act.wait_ge(g_window_done, w + 1)
                    nc.scalar.activation(k.ADJ[:, :, bass.ds(w * W, W)],
                                         counts[:, 0, 0:CODES].rearrange("p (t w) -> p t w", w=W),
                                         ACT.Copy, scale=UNIT).then_inc(g_stored, 1)
                act.wait_ge(g_stored, NW + 1)

        @block.sync
        def _(sp):
            load_windows(sp, 0, 0, LW // 2 // LOADS_AT_ONCE, LOADS_AT_ONCE)
            for load in range(1, LOADS):
                load_windows(sp, load, 0, LW // LOADS_AT_ONCE, LOADS_AT_ONCE)
            sp.wait_ge(flag_ready, 1)
            again = sp.value_load(missed[0:1, 0:1], min_val=0, max_val=1)
            with sp.If(again):
                sp.dma_start(window_keys[0:EP, 0:EF], d.keys.rearrange("(p f) -> p f", p=EP)).then_inc(g_keys_in, 16)
                sp.wait_ge(g_keys_in, 16)


PARTS = 2
SCALE = 2048.0
ONE = PARTS * C
YC = ONE + 2
CHUNK = 4
CW = CHUNK * P
BIG = 3.0e38
BN_EPS = GN_EPS = 1e-5


def tiles(ap, g, n=G):
    return ap[:, g * n:(g + 1) * n, :] if isinstance(g, int) else ap[:, bass.ds(g * n, n), :]


def group(ap, g):
    return ap[:, g * G:(g + 1) * G]


def across(ap):
    return ap.unsqueeze(2).to_broadcast([P, ap.shape[1], C])


def down(ap, n=NT):
    return ap.unsqueeze(1).to_broadcast([P, n, C])


def part(k, q, g):
    return tiles(k.Y, g)[:, :, q * C:(q + 1) * C]


def pe_aggregate(k, nc, pe, s, y_ready, reads, cols, after):
    def product(j, i):
        return nc.tensor.matmul(k.ps[:, j % G, 0:cols], k.ADJ[:, i, j * P:(j + 1) * P], k.Y[:, i, 0:cols],
                                start=i == 0, stop=i == NT - 1)

    for g in range(NG):
        pe.wait_ge(y_ready, g + 1)
        for j in range(G):
            for i in range(g * G, (g + 1) * G):
                last = product(j, i)
            if g == NG - 1:
                last.then_inc(s.summed, 1)
    for j in range(NT):
        if j >= G:
            pe.wait_ge(s.emptied, (j + 1 - G) * reads)
            for i in range(NT):
                last = product(j, i)
            last.then_inc(s.summed, 1)
        after(j)


def add_parts(nc, k, out, b):
    return nc.vector.tensor_reduce(out, k.ps[:, b, 0:ONE].rearrange("p (q f) -> p f q", q=PARTS), axis=AX, op=ALU.add)


def unscaled(nc, k, factor, g):
    return nc.vector.scalar_tensor_tensor(out=tiles(k.H, g), in0=tiles(k.H, g), scalar=1 / (SCALE * UNIT), in1=across(group(factor, g)),
                                          op0=ALU.mult, op1=ALU.mult)


def act_high(nc, k, g, high):
    nc.scalar.activation(part(k, 0, g), tiles(k.H, g), ACT.Copy, scale=SCALE).then_inc(high, 1)


def dve_low(nc, k, dve, g, high, y_ready):
    dve.wait_ge(high, g + 1)
    nc.vector.scalar_tensor_tensor(out=part(k, 1, g), in0=tiles(k.H, g), scalar=SCALE, in1=part(k, 0, g), op0=ALU.mult,
                                   op1=ALU.subtract).then_inc(y_ready, 1)



def dve_centre(nc, k, dve, chain, g, centred):
    mean = group(k.s1, g)
    chain(dve.tensor_reduce(mean, tiles(k.X, g), axis=AX, op=ALU.add))
    chain(dve.tensor_scalar(mean, mean, 1.0 / C, None, ALU.mult))
    dve.tensor_tensor(tiles(k.H, g), tiles(k.X, g), across(mean), ALU.subtract).then_inc(centred, 1)


def act_square(nc, k, act, g, centred, squared, read):
    act.wait_ge(centred, g + 1)
    if g >= 2:
        act.wait_ge(read, g - 1)
    nc.scalar.activation(k.T2[:, g % 2, :, :], tiles(k.H, g), ACT.Square).then_inc(squared, 1)


def dve_square_sum(k, dve, g, squared, read):
    dve.wait_ge(squared, g + 1)
    dve.tensor_reduce(group(k.s2, g), k.T2[:, g % 2, :, :], axis=AX, op=ALU.add).then_inc(read, 1)


def dve_normalise(nc, k, dve, chain, read, variance, deviation, done, factor=None, high=None, y_ready=None):
    dve.wait_ge(read, NG)
    dve.tensor_scalar(k.s1[:, :], k.s2[:, :], 1.0 / C, LN_EPS, ALU.mult, ALU.add).then_inc(variance, 1)
    dve.wait_ge(deviation, 1)
    chain(dve.reciprocal(k.s2[:, :], k.s2[:, :]))
    if factor is not None:
        chain(dve.tensor_tensor(k.s2[:, :], k.s2[:, :], factor, ALU.mult))
    for g in range(NG):
        nc.vector.scalar_tensor_tensor(out=tiles(k.H, g), in0=tiles(k.H, g), scalar=0.0, in1=across(group(k.s2, g)),
                                       op0=ALU.max, op1=ALU.mult).then_inc(done, 1)
        if high is not None and g >= 1:
            dve_low(nc, k, dve, g - 1, high, y_ready)
    if high is not None:
        dve_low(nc, k, dve, NG - 1, high, y_ready)


def act_deviation(nc, k, act, variance, deviation):
    act.wait_ge(variance, 1)
    nc.scalar.activation(k.s2[:, :], k.s1[:, :], ACT.Sqrt).then_inc(deviation, 1)


def pe_column_sums(nc, k, pe, ready, of, out, g):
    pe.wait_ge(ready, g + 1)
    for t in range(g * G, (g + 1) * G):
        rows = P if t < NT - 1 else LAST
        last = nc.tensor.matmul(out, k.ones[0:rows, :], of[0:rows, t, :], start=t == 0, stop=t == NT - 1)
    return last


def load_rows(sp, loads, done):
    for to, of in loads:
        if len(of.shape) == 1:
            of = of.rearrange("(a f) -> a f", a=1).to_broadcast([P, C])
        sp.dma_start(to[:, :], of).then_inc(done, 16)


def convolutions(nc, k, d, c, block):
    s = semaphores(nc, k, "c1", "chain vectors centred clipped root value high "
                   "y_ready summed emptied in_clipped in_root h_ready sums_ready centred_h squared_h squares_ready "
                   "var_h dev_h scaled affine gated")
    u = semaphores(nc, k, "c2", "value high y_ready summed emptied centred squared read variance deviation normal next_high next_y")
    bias, bias2, gamma, beta, mean, scale, shift = (
        c.enter_context(nc.sbuf_tensor(f"c1_{n}", [P, C], F32)) for n in "bias bias2 gamma beta mean scale shift".split())
    sums, squares = k.ps[:, 5, 0:C], k.ps[:, 6, 0:C]
    k.y_ready = u.next_y

    @block.sync
    def _(sp):
        load_rows(sp, [(bias, d.bias1), (gamma, d.gamma), (beta, d.beta), (bias2, d.bias2)], s.vectors)
        sp.wait_ge(s.vectors, 4 * 16)

    @block.vector
    def _(dve):
        chain = Chain(dve, s.chain)
        chain(dve.tensor_scalar(k.clipped[:, 0, :], k.out_deg[:, :], 1.0, None, ALU.max))
        dve.tensor_tensor(k.clipped[:, 1, :], k.clipped[:, 0, :], k.var0[:, :], ALU.mult).then_inc(s.clipped, 1)
        for g in range(NG):
            dve.tensor_tensor(tiles(k.H, g), tiles(k.X, g), across(group(k.mean0, g)), ALU.subtract).then_inc(s.centred, 1)
        chain(dve.memset(k.Y[:, :, ONE:YC], 1 / UNIT))
        dve.wait_ge(s.root, 1)
        chain(dve.reciprocal(k.roots[:, :, :], k.roots[:, :, :]))
        dve.wait_ge(s.centred, NG)
        for g in range(NG):
            nc.vector.scalar_tensor_tensor(out=tiles(k.H, g), in0=tiles(k.H, g), scalar=0.0,
                                           in1=across(group(k.roots[:, 1, :], g)),
                                           op0=ALU.max, op1=ALU.mult).then_inc(s.value, 1)
            if g >= 1:
                dve_low(nc, k, dve, g - 1, s.high, s.y_ready)
        dve_low(nc, k, dve, NG - 1, s.high, s.y_ready)
        chain(nc.vector.scalar_tensor_tensor(out=k.dis[:, :], in0=k.out_deg[:, :], scalar=1.0, in1=k.out_norm,
                                             op0=ALU.min, op1=ALU.mult))

        def degrees(g):
            dve.wait_ge(s.emptied, 2 * G * (g + 1))
            chain(dve.tensor_scalar(group(k.in_deg, g), group(k.in_deg, g), 1.0, None, ALU.max))
            dve.reciprocal(group(k.inv_deg, g), group(k.in_deg, g)).then_inc(s.in_clipped, 1)

        def finish(g):
            dve.wait_ge(s.in_root, g + 1)
            chain(dve.reciprocal(group(k.in_norm, g), group(k.in_norm, g)))
            chain(unscaled(nc, k, k.in_norm, g))
            dve.tensor_tensor(tiles(k.H, g), tiles(k.H, g), down(bias[:, :], G), ALU.add).then_inc(s.h_ready, 1)

        dve.wait_ge(s.vectors, 4 * 16)
        for j in range(NT):
            dve.wait_ge(s.summed, j + 1)
            add_parts(nc, k, tiles(k.H, j, 1), j % G).then_inc(s.emptied, 1)
            nc.vector.tensor_copy(k.in_deg[:, j:j + 1], k.ps[:, j % G, ONE:ONE + 1]).then_inc(s.emptied, 1)
            if j % G == G - 1:
                degrees(j // G)
            if j % G == 1 and j > G:
                finish(j // G - 1)
        finish(NG - 1)
        dve.wait_ge(s.sums_ready, 1)
        chain(dve.tensor_scalar(mean[:, :], sums, 1.0 / N, None, ALU.mult))
        for g in range(NG):
            dve.tensor_tensor(tiles(k.H, g), tiles(k.H, g), down(mean[:, :], G), ALU.subtract).then_inc(s.centred_h, 1)
        dve.wait_ge(s.squares_ready, 1)
        dve.tensor_scalar(scale[:, :], squares, 1.0 / N, BN_EPS, ALU.mult, ALU.add).then_inc(s.var_h, 1)
        dve.wait_ge(s.dev_h, 1)
        chain(dve.reciprocal(scale[:, :], shift[:, :]))
        chain(dve.tensor_tensor(scale[:, :], scale[:, :], gamma[:, :], ALU.mult))

        def scaled(g):
            dve.tensor_tensor(tiles(k.H, g), tiles(k.H, g), down(scale[:, :], G), ALU.mult).then_inc(s.scaled, 1)

        scaled(0)
        for g in range(NG):
            if g + 1 < NG:
                scaled(g + 1)
            dve.wait_ge(s.scaled, g + 1)
            dve.tensor_tensor(tiles(k.H, g), tiles(k.H, g), down(beta[:, :], G), ALU.add).then_inc(s.affine, 1)
        for g in range(NG):
            dve_low(nc, k, dve, g, u.high, u.y_ready)

        chain(dve.tensor_tensor(k.X[:, :, :], k.X[:, :, :], down(bias2[:, :]), ALU.add))

        def residual(g):
            dve.wait_ge(u.emptied, G * (g + 1))
            chain(unscaled(nc, k, k.in_norm, g))
            chain(dve.tensor_tensor(tiles(k.X, g), tiles(k.X, g), tiles(k.H, g), ALU.add))
            dve_centre(nc, k, dve, chain, g, u.centred)
            if g >= 1:
                dve_square_sum(k, dve, g - 1, u.squared, u.read)

        for j in range(NT):
            dve.wait_ge(u.summed, j + 1)
            add_parts(nc, k, tiles(k.H, j, 1), j % G).then_inc(u.emptied, 1)
            if j % G == G - 1:
                residual(j // G)
        dve_square_sum(k, dve, NG - 1, u.squared, u.read)
        dve_normalise(nc, k, dve, chain, u.read, u.variance, u.deviation, u.normal, None, u.next_high, u.next_y)

    @block.gpsimd
    def _(pool):
        for g in range(NG):
            pool.wait_ge(s.gated, g + 1)
            pool.tensor_tensor(tiles(k.H, g), tiles(k.H, g), across(group(k.out_norm, g)), ALU.mult).then_inc(u.value, 1)

    @block.scalar
    def _(act):
        act.wait_ge(s.clipped, 1)
        nc.scalar.activation(k.roots[:, :, :], k.clipped[:, :, :], ACT.Sqrt).then_inc(s.root, 1)
        for g in range(NG):
            act.wait_ge(s.value, g + 1)
            act_high(nc, k, g, s.high)
        for g in range(NG):
            act.wait_ge(s.in_clipped, g + 1)
            nc.scalar.activation(group(k.in_norm, g), group(k.in_deg, g), ACT.Sqrt).then_inc(s.in_root, 1)
        for g in range(NG):
            act.wait_ge(s.centred_h, g + 1)
            nc.scalar.activation(tiles(k.T, g), tiles(k.H, g), ACT.Square).then_inc(s.squared_h, 1)
        act.wait_ge(s.var_h, 1)
        nc.scalar.activation(shift[:, :], scale[:, :], ACT.Sqrt).then_inc(s.dev_h, 1)
        for g in range(NG):
            act.wait_ge(s.affine, g + 1)
            nc.scalar.activation(tiles(k.H, g), tiles(k.H, g), ACT.Sigmoid).then_inc(s.gated, 1)
        for g in range(NG):
            act.wait_ge(u.value, g + 1)
            act_high(nc, k, g, u.high)
        for g in range(NG):
            act_square(nc, k, act, g, u.centred, u.squared, u.read)
        act_deviation(nc, k, act, u.variance, u.deviation)
        for g in range(NG):
            act.wait_ge(u.normal, g + 1)
            act_high(nc, k, g, u.next_high)

    @block.tensor
    def _(pe):
        def column_sums(j):
            if j % G == G - 2 and j > G:
                pe_column_sums(nc, k, pe, s.h_ready, k.H, sums, j // G - 1)

        pe_aggregate(k, nc, pe, s, s.y_ready, 2, ONE + 1, column_sums)
        pe_column_sums(nc, k, pe, s.h_ready, k.H, sums, NG - 1).then_inc(s.sums_ready, 1)
        for g in range(NG):
            last = pe_column_sums(nc, k, pe, s.squared_h, k.T, squares, g)
        last.then_inc(s.squares_ready, 1)
        pe_aggregate(k, nc, pe, u, u.y_ready, 1, ONE, lambda j: None)


def sage(nc, k, d, c, block):
    names = "high summed emptied scaled_a agg_ready turned copied product added "
    s = semaphores(nc, k, "sg1", names + "chain inputs parts_ready total_ready bound bound_root weights relu")
    u = semaphores(nc, k, "sg2", names + "y_ready biased centred squared read variance deviation normal stored")
    w1, w2 = (c.enter_context(nc.sbuf_tensor(f"sg_w{n}", [C, 2 * C], F32)) for n in (1, 2))
    b1, b2 = (c.enter_context(nc.sbuf_tensor(f"sg_b{n}", [P, C], F32)) for n in (1, 2))
    b1_column = c.enter_context(nc.sbuf_tensor("sg_b1_column", [C, 1], F32))
    w_squares = c.enter_context(nc.sbuf_tensor("sg_w_squares", [C, 2 * C], F32))
    parts = c.enter_context(nc.sbuf_tensor("sg_parts", [C, 2], F32))
    size = c.enter_context(nc.sbuf_tensor("sg_size", [P, 4], F32))
    A = c.enter_context(nc.sbuf_tensor("sg_sum", [P, 3, C], F32))
    HT = c.enter_context(nc.sbuf_tensor("sg_turned", [C, 2, 2 * P], F32))
    k.residual_stored, k.h_ready = u.stored, u.normal
    TURNED, PRODUCT = 5, 6

    @block.sync
    def _(sp):
        sp.dma_start(w1[:, 0:C], d.W_neigh1).then_inc(s.inputs, 16)
        sp.dma_start(w1[:, C:2 * C], d.W_self1).then_inc(s.inputs, 16)
        sp.dma_start(b1_column[:, :], d.b1.rearrange("(f a) -> f a", a=1)).then_inc(s.inputs, 16)
        load_rows(sp, [(b1, d.b1), (b2, d.b2)], s.inputs)
        sp.dma_start(w2[:, 0:C], d.W_neigh2).then_inc(s.inputs, 16)
        sp.dma_start(w2[:, C:2 * C], d.W_self2).then_inc(s.inputs, 16)
        for g in range(NG):
            sp.wait_ge(u.normal, g + 1)
            sp.dma_start(tiles(d.residual, g), tiles(k.H, g)).then_inc(u.stored, 16)
        sp.wait_ge(s.inputs, 7 * 16)

    @block.vector
    def _(dve):
        chain = Chain(dve, s.chain)
        dve.wait_ge(s.inputs, 7 * 16)
        chain(dve.tensor_tensor(w_squares[:, :], w1[:, :], w1[:, :], ALU.mult))
        chain(dve.tensor_reduce(parts[:, 0:1], w_squares[:, :], axis=AX, op=ALU.add))
        chain(dve.tensor_tensor(parts[:, 1:2], b1_column[:, :], b1_column[:, :], ALU.mult))
        nc.vector.scalar_tensor_tensor(out=parts[:, 0:1], in0=parts[:, 0:1], scalar=2.0 * C, in1=parts[:, 1:2],
                                       op0=ALU.mult, op1=ALU.add).then_inc(s.parts_ready, 1)
        dve.wait_ge(s.total_ready, 1)
        dve.tensor_scalar(size[:, 0:1], k.ps[:, PRODUCT, 0:1], 2.0, 1e-30, ALU.mult, ALU.add).then_inc(s.bound, 1)
        dve.wait_ge(s.bound_root, 1)
        chain(dve.reciprocal(size[:, 2:3], size[:, 1:2]))
        chain(dve.tensor_scalar(b1[:, :], b1[:, :], size[:, 2:3], None, ALU.mult))
        dve.tensor_scalar(w1[:, :], w1[:, :], size[0:C, 2:3], None, ALU.mult).then_inc(s.weights, 1)
        dve.tensor_scalar(w2[:, :], w2[:, :], size[0:C, 1:2], None, ALU.mult).then_inc(s.weights, 1)

        def mean_of(j, v):
            out = A[:, j % 3, :]
            dve.wait_ge(v.summed, j + 1)
            if j >= 3:
                dve.wait_ge(v.turned, j - 2)
            add_parts(nc, k, A[:, j % 3:j % 3 + 1, :], j % G).then_inc(v.emptied, 1)
            dve.wait_ge(v.emptied, j + 1)
            dve.tensor_scalar(out, out, k.inv_deg[:, j:j + 1], 1 / (SCALE * UNIT), ALU.mult, ALU.mult).then_inc(v.agg_ready, 1)

        def output_1(j):
            dve.wait_ge(s.product, j + 1)
            dve.tensor_tensor(k.H[:, j, :], k.ps[:, PRODUCT + j % 2, 0:C], b1[:, :], ALU.add).then_inc(s.added, 1)

        for j in range(NT + 2):
            if j < NT:
                mean_of(j, s)
            if j >= 2:
                output_1(j - 2)
        for g in range(NG):
            dve_low(nc, k, dve, g, u.high, u.y_ready)
        dve.tensor_tensor(k.X[:, :, :], k.X[:, :, :], down(b2[:, :]), ALU.add).then_inc(u.biased, 1)
        dve.wait_ge(u.biased, 1)

        def output_2(j):
            dve.wait_ge(u.product, j + 1)
            dve.tensor_tensor(k.X[:, j, :], k.X[:, j, :], k.ps[:, PRODUCT + j % 2, 0:C], ALU.add).then_inc(u.added, 1)
            if j % G == G - 1:
                g = j // G
                dve.wait_ge(u.added, j + 1)
                dve_centre(nc, k, dve, chain, g, u.centred)
                if g >= 1:
                    dve_square_sum(k, dve, g - 1, u.squared, u.read)

        for j in range(NT + 2):
            if j < NT:
                mean_of(j, u)
            if j >= 2:
                output_2(j - 2)
        dve_square_sum(k, dve, NG - 1, u.squared, u.read)
        dve_normalise(nc, k, dve, chain, u.read, u.variance, u.deviation, u.normal)

    @block.scalar
    def _(act):
        act.wait_ge(s.bound, 1)
        nc.scalar.activation(size[:, 1:2], size[:, 0:1], ACT.Sqrt).then_inc(s.bound_root, 1)

        def copy_turned(j, v):
            act.wait_ge(v.turned, j + 1)
            if j >= 2:
                act.wait_ge(v.product, j - 1)
            nc.scalar.activation(HT[:, j % 2, :], k.ps[0:C, TURNED, 0:2 * P], ACT.Copy).then_inc(v.copied, 1)

        def relu(g):
            act.wait_ge(s.added, G * (g + 1))
            nc.scalar.activation(tiles(k.H, g), tiles(k.H, g), ACT.Relu).then_inc(s.relu, 1)

        for j in range(NT):
            copy_turned(j, s)
            if j % G == 3 and j > G:
                relu(j // G - 1)
        relu(NG - 1)
        act.wait_ge(s.summed, NT)
        act.wait_ge(s.relu, NG)
        for g in range(NG):
            act_high(nc, k, g, u.high)
        for j in range(NT):
            copy_turned(j, u)
            if j % G == 4 and j > G:
                act_square(nc, k, act, j // G - 1, u.centred, u.squared, u.read)
        act_square(nc, k, act, NG - 1, u.centred, u.squared, u.read)
        act_deviation(nc, k, act, u.variance, u.deviation)

    @block.tensor
    def _(pe):
        def turn(j, v):
            pe.wait_ge(v.agg_ready, j + 1)
            if j >= 1:
                pe.wait_ge(v.copied, j)
            nc.tensor.transpose(k.ps[0:C, TURNED, 0:P], A[:, j % 3, :], k.ident[:, :])
            nc.tensor.transpose(k.ps[0:C, TURNED, P:2 * P], k.H[:, j, :], k.ident[:, :]).then_inc(v.turned, 1)

        def multiply(j, v, w):
            pe.wait_ge(v.copied, j + 1)
            if j >= 2:
                pe.wait_ge(v.added, j - 1)
            bank = k.ps[:, PRODUCT + j % 2, 0:C]
            nc.tensor.matmul(bank, HT[:, j % 2, 0:P], w[:, 0:C], start=True, stop=False)
            nc.tensor.matmul(bank, HT[:, j % 2, P:2 * P], w[:, C:2 * C], start=False, stop=True).then_inc(v.product, 1)

        def step(v, w):
            def after(j):
                if j == 0 and v is s:
                    pe.wait_ge(s.parts_ready, 1)
                    nc.tensor.matmul(k.ps[:, PRODUCT, 0:1], k.ones[0:C, :], parts[:, 0:1], start=True,
                                     stop=True).then_inc(s.total_ready, 1)
                if 1 <= j <= NT:
                    turn(j - 1, v)
                if j == 2 and v is s:
                    pe.wait_ge(s.weights, 2)
                if j >= 2:
                    multiply(j - 2, v, w)
            return after

        for v, y_ready, w in ((s, k.y_ready, w1), (u, u.y_ready, w2)):
            after = step(v, w)
            pe_aggregate(k, nc, pe, v, y_ready, 1, ONE, after)
            after(NT)
            after(NT + 1)


def prepare_attention(nc, k, d, c, block, name, w, a_src, a_dst, first):
    s = semaphores(nc, k, name, "chain loads w_turned w_copied turned copied product emptied_d "
                   "extremes ex_turned ex_diag ex_rows")
    w_in = c.enter_context(nc.sbuf_tensor(f"{name}_w", [C, C], F32))
    a_in = c.enter_context(nc.sbuf_tensor(f"{name}_a", [C, 2], F32))
    weights = c.enter_context(nc.sbuf_tensor(f"{name}_weights", [C, C + 2], F32))
    ext = c.enter_context(nc.sbuf_tensor(f"{name}_ext", [P, 8], F32))
    HT = c.enter_context(nc.sbuf_tensor(f"{name}_HT", [C, 2, G * P], F32))

    def turned_banks(g):
        return flat(k.ps[0:C, g % 2 * 2:g % 2 * 2 + 2, :])[:, 0:G * P]


    @block.sync
    def _(sp):
        sp.dma_start(w_in[:, :], w).then_inc(s.loads, 16)
        sp.dma_start(a_in[:, 0:1], a_src.rearrange("(f a) -> f a", a=1)).then_inc(s.loads, 16)
        sp.dma_start(a_in[:, 1:2], a_dst.rearrange("(f a) -> f a", a=1)).then_inc(s.loads, 16)
        sp.wait_ge(s.loads, 48)
        if first:
            sp.wait_ge(k.residual_stored, NG * 16)

    @block.vector
    def _(dve):
        chain = Chain(dve, s.chain)
        if first:
            adj = flat(k.ADJ[:, :, :])
            most = adj[:, 0:(NT - 1) * (NP + P)].rearrange("p (t q) -> p t q", q=NP + P)[:, :, 0:P]
            chain(dve.tensor_tensor(most, most, k.loops_h[:, :].unsqueeze(1).to_broadcast([P, NT - 1, P]), ALU.add))
            end = adj[:, (NT - 1) * (NP + P):NT * NP]
            chain(dve.tensor_tensor(end, end, k.loops_h[:, :], ALU.add))
        dve.wait_ge(s.w_turned, 2)
        dve.tensor_copy(weights[:, 0:C], k.ps[0:C, 6, 0:C]).then_inc(s.w_copied, 1)
        dve.tensor_copy(weights[:, C:C + 2], k.ps[0:C, 7, 0:2]).then_inc(s.w_copied, 1)
        for g in range(NG):
            dve.wait_ge(s.product, g + 1)
            products = k.ps[:, 4 + g % 2, 0:G * (C + 2)].rearrange("p (t f) -> p t f", f=C + 2)
            dve.tensor_copy(tiles(k.Hg, g), products).then_inc(s.emptied_d, 1)
        dve.wait_ge(s.emptied_d, NG)
        chain(dve.tensor_copy(k.a_s[:, :], k.Hg[:, :, C]))
        chain(dve.tensor_copy(k.a_d[:, :], k.Hg[:, :, C + 1]))
        chain(dve.memset(k.Hg[:, :, C:C + 1], 1.0))
        chain(dve.tensor_scalar(k.a_s5[:, :], k.a_s[:, :], SLOPE, None, ALU.mult))
        chain(dve.tensor_scalar(k.s3[:, :], k.a_s[:, :], -1.0, None, ALU.mult))
        chain(dve.tensor_scalar(k.s2[:, :], k.a_d[:, :], -1.0, None, ALU.mult))
        chain(dve.tensor_tensor(k.s2[:, :], k.s2[:, :], k.a_d[:, :], ALU.max))
        chain(dve.tensor_reduce(ext[:, 0:1], k.a_s[:, :], axis=AX, op=ALU.max))
        chain(dve.tensor_reduce(ext[:, 1:2], k.s3[:, :], axis=AX, op=ALU.max))
        dve.tensor_reduce(ext[:, 2:3], k.s2[:, :], axis=AX, op=ALU.max).then_inc(s.extremes, 1)
        dve.wait_ge(s.ex_turned, 1)
        chain(dve.tensor_reduce(ext[0:3, 3:4], k.ps[0:3, 6, 0:P], axis=AX, op=ALU.max))
        dve.tensor_scalar(ext[0:3, 4:7], k.ident[0:3, 0:3], ext[0:3, 3:4], None, ALU.mult).then_inc(s.ex_diag, 1)
        dve.wait_ge(s.ex_rows, 1)
        chain(dve.tensor_copy(ext[:, 5:7], k.ps[:, 7, 0:2]))
        chain(dve.tensor_tensor(ext[:, 7:8], ext[:, 5:6], ext[:, 6:7], ALU.add))
        chain(dve.tensor_scalar(ext[:, 7:8], ext[:, 7:8], 1e-20, None, ALU.max))
        chain(dve.tensor_scalar(k.unscale[:, 0:1], ext[:, 7:8], 2.0, None, ALU.mult))
        chain(nc.vector.scalar_tensor_tensor(out=k.unscale[:, 1:2], in0=ext[:, 7:8], scalar=-1.0, in1=ext[:, 6:7],
                                             op0=ALU.mult, op1=ALU.subtract))
        chain(dve.reciprocal(ext[:, 5:6], k.unscale[:, 0:1]))
        chain(dve.tensor_scalar(k.a_unit[:, :], k.a_s[:, :], ext[:, 6:7], ext[:, 5:6], ALU.add, ALU.mult))
        chain(dve.tensor_scalar(k.a_unit[:, :], k.a_unit[:, :], 0.5, UNIT, ALU.add, ALU.mult))
        chain(dve.tensor_scalar(k.unscale[:, 0:1], k.unscale[:, 0:1], 1 / UNIT, None, ALU.mult))
        chain(dve.tensor_reduce(ext[0:1, 0:1], k.ps[0:1, 7, 0:3], axis=AX, op=ALU.max))
        chain(dve.tensor_scalar(k.wide[0:1, 0:1], ext[0:1, 0:1], SMALL, None, ALU.is_gt))

    @block.scalar
    def _(act):
        act.preload_act_table(ACT.Copy)
        for g in range(NG):
            act.wait_ge(s.turned, g + 1)
            if g >= 2:
                act.wait_ge(s.product, g - 1)
            nc.scalar.activation(HT[:, g % 2, :], turned_banks(g), ACT.Copy).then_inc(s.copied, 1)

    @block.tensor
    def _(pe):
        pe.wait_ge(s.loads, 48)
        pe.wait_ge(k.h_ready, 1)
        nc.tensor.transpose(k.ps[0:C, 6, 0:C], w_in[:, :], k.ident[0:C, 0:C]).then_inc(s.w_turned, 1)
        nc.tensor.matmul(k.ps[0:C, 7, 0:2], w_in[:, :], a_in[:, :], start=True, stop=True).then_inc(s.w_turned, 1)

        def turn(g):
            pe.wait_ge(k.h_ready, g + 1)
            if g >= 2:
                pe.wait_ge(s.copied, g - 1)
            for t in range(G):
                last = nc.tensor.transpose(turned_banks(g)[:, t * P:(t + 1) * P], k.H[:, g * G + t, :], k.ident[:, :])
            last.then_inc(s.turned, 1)

        def multiply(g):
            pe.wait_ge(s.copied, g + 1)
            if g == 0:
                pe.wait_ge(s.w_copied, 2)
            if g >= 2:
                pe.wait_ge(s.emptied_d, g - 1)
            for t in range(G):
                last = nc.tensor.matmul(k.ps[:, 4 + g % 2, t * (C + 2):(t + 1) * (C + 2)], HT[:, g % 2, t * P:(t + 1) * P],
                                        weights[:, :], start=True, stop=True)
            last.then_inc(s.product, 1)

        for g in range(NG + 1):
            if g < NG:
                turn(g)
            if g >= 1:
                multiply(g - 1)
        pe.wait_ge(s.extremes, 1)
        nc.tensor.transpose(k.ps[0:3, 6, 0:P], ext[:, 0:3], k.ident[:, :]).then_inc(s.ex_turned, 1)
        pe.wait_ge(s.ex_diag, 1)
        nc.tensor.matmul(k.ps[:, 7, 0:3], k.ones[0:3, :], ext[0:3, 4:7], start=True, stop=True).then_inc(s.ex_rows, 1)


SLOPE = 0.2
NC = NT // CHUNK
REST = NT % CHUNK
MAX_STEPS, SHIFT_STEPS = NT, 5
ACC, TURN, ROWS_U, ROWS_V, OUT, OTHER_OUT = 0, 1, 2, 3, 6, 0
EXPS = (4, 5, 7)
SMALL = 30.0
RING4 = [i % 4 if i < NT - 9 else (i - NT + 9) % 3 for i in range(NT)]


def attend(nc, k, d, name, b):
    with ExitStack() as c:
        s = semaphores(nc, k, name, "chain max_ready max_turned uv_ready diag_ready rows_ready exp_ready prob_ready "
                       "used out_ready out_copied out_turned h_written small bias_in summed")
        t = semaphores(nc, k, name + "b", "factor hg_ready diag_ready rows_ready exp_ready prob_ready used "
                       "out_copied out_turned norm_ready h_written summed")
        work = c.enter_context(nc.sbuf_tensor(f"{name}_work", [P, 7, CW], F32))
        prob, odd, exp_v, ring = work[:, 0:2, :], work[:, 2, :], work[:, 3:6, :], work[:, 0:4, :]
        out_sb = work[:, 6, :]
        peak = c.enter_context(nc.sbuf_tensor(f"{name}_peak", [P, CHUNK], F32))
        bias = c.enter_context(nc.sbuf_tensor(f"{name}_bias", [P, C], F32))
        u = c.enter_context(nc.sbuf_tensor(f"{name}_u", [P, CHUNK], F32))
        v = c.enter_context(nc.sbuf_tensor(f"{name}_v", [P, CHUNK], F32))
        rz = c.enter_context(nc.sbuf_tensor(f"{name}_rz", [P, CHUNK], F32))
        block = c.enter_context(nc.Block())
        diag = k.spare[:, 0:2 * CW].rearrange("p (a q) -> p a q", a=2)

        def cols(ch, n):
            return slice(ch * CW, ch * CW + n * P) if isinstance(ch, int) else bass.ds(ch * CW, n * P)

        def nodes(ch, n):
            return slice(ch * CHUNK, ch * CHUNK + n) if isinstance(ch, int) else bass.ds(ch * CHUNK, n)

        def column_sums(dve, ch, n, h_written, summed, of=range(CHUNK)):
            if n == CHUNK:
                dve.wait_ge(h_written, ch + 1)
                for i in of:
                    dve.wait_ge(summed, ch * CHUNK + (i + 1))
                    tile = flat(k.H[:, bass.ds(ch * CHUNK + i, 1), :])
                    dve.tensor_tensor(k.column_sums, k.column_sums, tile, ALU.add).then_inc(summed, 1)

        def exact_vector(dve):
            chain = Chain(dve, s.chain)

            def maxima(ch, n):
                acc = (k.ps[:, ACC, 0:n * P], odd[:, 0:n * P])
                for i in range(NT):
                    counts = k.ADJ[:, i, cols(ch, n)]
                    if i < 2:
                        chain.lag(dve.tensor_scalar(acc[i], counts, k.a_unit[:, i:i + 1], None, ALU.min))
                    else:
                        chain.lag(nc.vector.scalar_tensor_tensor(out=acc[i % 2], in0=counts, scalar=k.a_unit[:, i:i + 1],
                                                                 in1=acc[i % 2], op0=ALU.min, op1=ALU.max))
                chain.all()
                dve.tensor_tensor(acc[1], acc[0], acc[1], ALU.max).then_inc(s.max_ready, 1)

            def shifts(ch, n):
                dve.wait_ge(s.max_turned, ch + 1)
                ad, pk, uu, vv = k.a_d[:, nodes(ch, n)], peak[:, 0:n], u[:, 0:n], v[:, 0:n]
                chain(dve.tensor_reduce(pk, k.ps[:, TURN, 0:n * P].rearrange("p (b q) -> p b q", q=P), axis=AX, op=ALU.max))
                chain(dve.tensor_scalar(pk, pk, k.unscale[:, 0:1], k.unscale[:, 1:2], ALU.mult, ALU.add))
                chain(dve.tensor_tensor(pk, pk, ad, ALU.add))
                chain(nc.vector.scalar_tensor_tensor(out=pk, in0=pk, scalar=SLOPE, in1=pk, op0=ALU.mult, op1=ALU.max))
                chain(dve.tensor_tensor(uu, ad, pk, ALU.subtract))
                nc.vector.scalar_tensor_tensor(out=vv, in0=ad, scalar=SLOPE, in1=pk, op0=ALU.mult,
                                               op1=ALU.subtract).then_inc(s.uv_ready, 1)

            def larger(ch, i, n):
                e = i % len(EXPS)
                dve.wait_ge(s.exp_ready, ch * NT + (i + 1))
                bank = k.ps[:, EXPS[e], 0:n * P]
                dve.tensor_tensor(bank, bank, exp_v[:, e, 0:n * P], ALU.max).then_inc(s.small, 1)

            def probabilities(ch, first, n):
                larger(ch, 0, n)
                for i in range(NT):
                    if i + 1 < NT:
                        larger(ch, i + 1, n)
                    dve.wait_ge(s.small, ch * NT + (i + 1))
                    if not first or i >= 2:
                        dve.wait_ge(s.used, ch * NT + (i - 1))
                    nc.vector.scalar_tensor_tensor(out=prob[:, i % 2, 0:n * P], in0=k.ps[:, EXPS[i % len(EXPS)], 0:n * P],
                                                   scalar=BIG, in1=k.ADJ[:, i, cols(ch, n)], op0=ALU.min,
                                                   op1=ALU.mult).then_inc(s.prob_ready, 1)

            def write(ch, n):
                dve.wait_ge(s.out_turned, ch + 1)
                sums = k.ps[:, TURN, 0:n * (C + 1)].rearrange("p (b q) -> p b q", q=C + 1)
                chain(dve.reciprocal(rz[:, 0:n], sums[:, :, C]))
                out = k.H[:, nodes(ch, n), :]
                chain(dve.tensor_tensor(out, sums[:, :, 0:C], rz[:, 0:n].unsqueeze(2).to_broadcast([P, n, C]), ALU.mult))
                dve.wait_ge(s.bias_in, 16)
                dve.tensor_tensor(out, out, down(bias[:, :], n), ALU.add).then_inc(s.h_written, 1)
                column_sums(dve, ch, n, s.h_written, s.summed)

            dve.memset(k.column_sums, 0.0).then_inc(s.summed, 1)
            maxima(0, CHUNK)
            shifts(0, CHUNK)
            maxima(1, CHUNK)
            probabilities(0, True, CHUNK)
            with dve.Fori(0, NC - 2) as r:
                chain.loop(r, MAX_STEPS + SHIFT_STEPS + 2)
                shifts(r + 1, CHUNK)
                maxima(r + 2, CHUNK)
                write(r, CHUNK)
                probabilities(r + 1, False, CHUNK)
            chain.end(NC - 2)
            shifts(NC - 1, CHUNK)
            maxima(NC, REST)
            write(NC - 2, CHUNK)
            probabilities(NC - 1, False, CHUNK)
            shifts(NC, REST)
            write(NC - 1, CHUNK)
            probabilities(NC, False, REST)
            write(NC, REST)
            dve.wait_ge(s.h_written, NC + 1)
            dve.wait_ge(s.summed, NC * CHUNK + 1)

        def exact_gpsimd(pool):
            def diagonals(ch, n):
                pool.wait_ge(s.uv_ready, ch + 1)
                for a, of in ((0, u), (1, v)):
                    pool.tensor_tensor(diag[:, a, 0:n * P].rearrange("p (b q) -> p b q", q=P),
                                       k.ident[:, :].unsqueeze(1).to_broadcast([P, n, P]),
                                       of[:, 0:n].unsqueeze(2).to_broadcast([P, n, P]), ALU.mult).then_inc(s.diag_ready, 1)

            with pool.Fori(0, NC) as ch:
                diagonals(ch, CHUNK)
            diagonals(NC, REST)

        def exact_scalar(act):
            def exponentials(ch, first, n):
                act.wait_ge(s.rows_ready, ch + 1)
                for i in range(NT):
                    e = i % len(EXPS)
                    if i >= len(EXPS):
                        act.wait_ge(s.prob_ready, ch * NT + (i + 1 - len(EXPS)))
                    elif not first:
                        act.wait_ge(s.prob_ready, ch * NT)
                    nc.scalar.activation(k.ps[:, EXPS[e], 0:n * P], k.ps[:, ROWS_U, 0:n * P], ACT.Exp, bias=k.a_s[:, i:i + 1])
                    nc.scalar.activation(exp_v[:, e, 0:n * P], k.ps[:, ROWS_V, 0:n * P], ACT.Exp,
                                         bias=k.a_s5[:, i:i + 1]).then_inc(s.exp_ready, 1)
                act.wait_ge(s.out_ready, ch + 1)
                nc.scalar.activation(out_sb[0:C + 1, 0:n * P], k.ps[0:C + 1, OUT, 0:n * P], ACT.Copy).then_inc(s.out_copied, 1)

            exponentials(0, True, CHUNK)
            with act.Fori(0, NC - 1) as r:
                exponentials(r + 1, False, CHUNK)
            exponentials(NC, False, REST)

        def exact_tensor(pe):
            def turn_maxima(ch, first, n):
                pe.wait_ge(s.max_ready, ch + 1)
                if not first:
                    pe.wait_ge(s.h_written, ch - 1)
                for b in range(n):
                    last = nc.tensor.transpose(k.ps[:, TURN, b * P:(b + 1) * P], odd[:, b * P:(b + 1) * P], k.ident[:, :])
                last.then_inc(s.max_turned, 1)

            def rows(ch, first, n):
                pe.wait_ge(s.diag_ready, ch * 2 + 2)
                if not first:
                    pe.wait_ge(s.exp_ready, ch * NT)
                nc.tensor.matmul(k.ps[:, ROWS_U, 0:n * P], k.ones[:, :], diag[:, 0, 0:n * P], start=True, stop=True)
                nc.tensor.matmul(k.ps[:, ROWS_V, 0:n * P], k.ones[:, :], diag[:, 1, 0:n * P], start=True,
                                 stop=True).then_inc(s.rows_ready, 1)

            def turn_output(ch, n):
                pe.wait_ge(s.out_copied, ch + 1)
                for b in range(n):
                    last = nc.tensor.transpose(k.ps[:, TURN, b * (C + 1):(b + 1) * (C + 1)],
                                               out_sb[0:C + 1, b * P:(b + 1) * P], k.ident[0:C + 1, 0:C + 1])
                last.then_inc(s.out_turned, 1)

            def products(ch, n):
                for i in range(NT):
                    pe.wait_ge(s.prob_ready, ch * NT + (i + 1))
                    nc.tensor.matmul(k.ps[0:C + 1, OUT, 0:n * P], k.Hg[:, i, 0:C + 1], prob[:, i % 2, 0:n * P],
                                     start=i == 0, stop=i == NT - 1).then_inc(s.used, 1)
                pe.wait_ge(s.used, (ch + 1) * NT)
                pe.sem_inc(s.out_ready, 1)

            turn_maxima(0, True, CHUNK)
            rows(0, True, CHUNK)
            products(0, CHUNK)
            turn_maxima(1, True, CHUNK)
            rows(1, False, CHUNK)
            turn_output(0, CHUNK)
            products(1, CHUNK)
            with pe.Fori(0, NC - 2) as r:
                turn_maxima(r + 2, False, CHUNK)
                rows(r + 2, False, CHUNK)
                turn_output(r + 1, CHUNK)
                products(r + 2, CHUNK)
            turn_maxima(NC, False, REST)
            rows(NC, False, REST)
            turn_output(NC - 1, CHUNK)
            products(NC, REST)
            pe.wait_ge(s.h_written, NC)
            turn_output(NC, REST)

        banks = (3, 4, 5, 7)
        outs = (OUT, OTHER_OUT)

        def slot_free(eng, sem, ch, i, first):
            last = max((j for j in range(i) if RING4[j] == RING4[i]), default=None)
            if last is not None:
                eng.wait_ge(sem, ch * NT + (last + 1))
            elif not first:
                last = max(j for j in range(NT) if RING4[j] == RING4[i])
                eng.wait_ge(sem, ch * NT + (last + 1 - NT))

        def chunks(eng, body):
            body(0, 0, CHUNK, 0)
            body(1, 1, CHUNK, 1)
            with eng.Fori(1, NC // 2) as r:
                body(r * 2, 2, CHUNK, 0)
                body(r * 2 + 1, 2, CHUNK, 1)
            body(NC, 2, REST, 0)

        def small_vector(dve):
            dve.tensor_scalar(k.s1[:, :], k.a_s[:, :], 1 - SLOPE, None, ALU.mult).then_inc(t.factor, 1)

            def write(ch, n):
                dve.wait_ge(t.out_turned, ch + 1)
                sums = k.ps[:, TURN, 0:n * (C + 1)].rearrange("p (b q) -> p b q", q=C + 1)
                dve.reciprocal(rz[:, 0:n], sums[:, :, C]).then_inc(t.norm_ready, 1)
                dve.wait_ge(t.norm_ready, ch * 2 + 1)
                out = k.H[:, nodes(ch, n), :]
                dve.tensor_tensor(out, sums[:, :, 0:C], rz[:, 0:n].unsqueeze(2).to_broadcast([P, n, C]),
                                  ALU.mult).then_inc(t.norm_ready, 1)
                dve.wait_ge(t.norm_ready, ch * 2 + 2)
                dve.wait_ge(s.bias_in, 16)
                dve.tensor_tensor(out, out, down(bias[:, :], n), ALU.add).then_inc(t.h_written, 1)

            def probabilities(ch, number, n, out):
                for i in range(NT):
                    dve.wait_ge(t.exp_ready, ch * NT + (i + 1))
                    slot_free(dve, t.used, ch, i, number == 0)
                    nc.vector.scalar_tensor_tensor(out=ring[:, RING4[i], 0:n * P], in0=k.ps[:, banks[RING4[i]], 0:n * P], scalar=1.0,
                                                   in1=k.ADJ[:, i, cols(ch, n)], op0=ALU.max,
                                                   op1=ALU.mult).then_inc(t.prob_ready, 1)
                    if i == 16 and number > 0:
                        write(ch - 1, CHUNK)
                    if i >= 18 and i % 2 == 0 and number > 0:
                        column_sums(dve, ch - 1, CHUNK, t.h_written, t.summed, [(i - 18) // 2])

            dve.memset(k.column_sums, 0.0).then_inc(t.summed, 1)
            chunks(dve, probabilities)
            write(NC, REST)
            dve.wait_ge(t.h_written, NC + 1)
            dve.wait_ge(t.summed, NC * CHUNK + 1)

        def small_gpsimd(pool):
            def diagonal(ch, number, n, out):
                if number > 0:
                    pool.wait_ge(t.rows_ready, ch)
                pool.tensor_tensor(diag[:, 0, 0:n * P].rearrange("p (b q) -> p b q", q=P),
                                   k.ident[:, :].unsqueeze(1).to_broadcast([P, n, P]),
                                   k.a_d[:, nodes(ch, n)].unsqueeze(2).to_broadcast([P, n, P]), ALU.mult).then_inc(t.diag_ready, 1)
                if number == 0:
                    pool.wait_ge(t.factor, 2)
                    for g in range(NG):
                        pool.tensor_tensor(tiles(k.Hg, g)[:, :, 0:C + 1], tiles(k.Hg, g)[:, :, 0:C + 1],
                                           group(k.s2, g).unsqueeze(2).to_broadcast([P, G, C + 1]), ALU.mult).then_inc(t.hg_ready, 1)

            chunks(pool, diagonal)

        def small_scalar(act):
            nc.scalar.activation(k.s2[:, :], k.a_s[:, :], ACT.Exp, scale=SLOPE).then_inc(t.factor, 1)
            act.wait_ge(t.factor, 2)

            def copy_out(ch, number, n, out):
                act.wait_ge(t.used, ch * NT + NT)
                if number > 0:
                    act.wait_ge(t.out_turned, ch)
                nc.scalar.activation(out_sb[0:C + 1, 0:n * P], k.ps[0:C + 1, outs[out], 0:n * P], ACT.Copy).then_inc(t.out_copied, 1)

            def exponentials(ch, number, n, out):
                act.wait_ge(t.rows_ready, ch + 1)
                for i in range(NT):
                    slot_free(act, t.prob_ready, ch, i, number == 0)
                    nc.scalar.activation(k.ps[:, banks[RING4[i]], 0:n * P], k.ps[:, ROWS_U, 0:n * P], ACT.Exp,
                                         bias=k.s1[:, i:i + 1], scale=1 - SLOPE).then_inc(t.exp_ready, 1)
                    if i == 6 and number > 0:
                        copy_out(ch - 1, number - 1, CHUNK, 1 - out)

            chunks(act, exponentials)
            copy_out(NC, 2, REST, 0)

        def small_tensor(pe):
            def rows(ch, first, n):
                pe.wait_ge(t.diag_ready, ch + 1)
                if not first:
                    pe.wait_ge(t.exp_ready, ch * NT)
                nc.tensor.matmul(k.ps[:, ROWS_U, 0:n * P], k.ones[:, :], diag[:, 0, 0:n * P], start=True,
                                 stop=True).then_inc(t.rows_ready, 1)

            def turn_output(ch, number, n):
                pe.wait_ge(t.out_copied, ch + 1)
                if number > 0:
                    pe.wait_ge(t.h_written, ch)
                for b in range(n):
                    last = nc.tensor.transpose(k.ps[:, TURN, b * (C + 1):(b + 1) * (C + 1)],
                                               out_sb[0:C + 1, b * P:(b + 1) * P], k.ident[0:C + 1, 0:C + 1])
                last.then_inc(t.out_turned, 1)

            def products(ch, number, n, out, following=CHUNK):
                if number > 1:
                    pe.wait_ge(t.out_copied, ch - 1)
                for i in range(NT):
                    if i == NT - 4 and following:
                        rows(ch + 1, False, following)
                    if number == 0 and i % G == 0:
                        pe.wait_ge(t.hg_ready, i // G + 1)
                    pe.wait_ge(t.prob_ready, ch * NT + (i + 1))
                    nc.tensor.matmul(k.ps[0:C + 1, outs[out], 0:n * P], k.Hg[:, i, 0:C + 1], ring[:, RING4[i], 0:n * P],
                                     start=i == 0, stop=i == NT - 1).then_inc(t.used, 1)
                    if i == 10 and number > 0:
                        turn_output(ch - 1, number - 1, CHUNK)

            rows(0, True, CHUNK)
            products(0, 0, CHUNK, 0)
            products(1, 1, CHUNK, 1)
            with pe.Fori(1, NC // 2 - 1) as r:
                products(r * 2, 2, CHUNK, 0)
                products(r * 2 + 1, 2, CHUNK, 1)
            products(NC - 2, 2, CHUNK, 0)
            products(NC - 1, 2, CHUNK, 1, REST)
            products(NC, 2, REST, 0, 0)
            turn_output(NC, 2, REST)

        @block.sync
        def _(sp):
            load_rows(sp, [(bias, b)], s.bias_in)
            sp.wait_ge(s.bias_in, 16)

        @block.vector
        def _(dve):
            wide = dve.value_load(k.wide[0:1, 0:1], min_val=0, max_val=1)
            with dve.If(wide):
                exact_vector(dve)
            with dve.Else():
                small_vector(dve)

        @block.gpsimd
        def _(pool):
            wide = pool.value_load(k.wide[0:1, 0:1], min_val=0, max_val=1)
            with pool.If(wide):
                exact_gpsimd(pool)
            with pool.Else():
                small_gpsimd(pool)

        @block.scalar
        def _(act):
            wide = act.value_load(k.wide[0:1, 0:1], min_val=0, max_val=1)
            act.preload_act_table(ACT.Exp)
            with act.If(wide):
                exact_scalar(act)
            with act.Else():
                small_scalar(act)

        @block.tensor
        def _(pe):
            wide = pe.value_load(k.wide[0:1, 0:1], min_val=0, max_val=1)
            with pe.If(wide):
                exact_tensor(pe)
            with pe.Else():
                small_tensor(pe)


def graph_norm(nc, k, d, c, block, name, last):
    s = semaphores(nc, k, name, "chain vectors sums_ready centred_h squared_h squares_ready var_h dev_h "
                   "first second third fourth fifth centred squared read variance deviation normal high y_ready loops_gone back shifted")
    weight, beta, mscale, mean, scale, dev = (
        c.enter_context(nc.sbuf_tensor(f"{name}_{n}", [P, C], F32)) for n in "weight beta mscale mean scale dev".split())
    if last:
        R = k.R = c.enter_context(nc.sbuf_tensor(f"{name}_R", [P, NT, C], F32))
    sums, squares = k.ps[:, 5, 0:C], k.ps[:, 6, 0:C]
    k.h_ready, k.y_ready, k.loops_gone = s.third, s.y_ready, s.loops_gone

    @block.sync
    def _(sp):
        load_rows(sp, [(weight, d.gn_weight), (beta, d.gn_bias), (mscale, d.gn_mean_scale)], s.vectors)
        if last:
            sp.dma_start(R[:, :, :], d.residual).then_inc(s.back, 16)
            sp.wait_ge(s.back, 16)
        sp.wait_ge(s.vectors, 3 * 16)

    @block.gpsimd
    def _(pool):
        if not last:
            pool.wait_ge(s.vectors, 3 * 16)
            for g in range(NG):
                pool.wait_ge(s.first, g + 1)
                pool.tensor_tensor(tiles(k.H, g), tiles(k.H, g), down(beta[:, :], G), ALU.add).then_inc(s.second, 1)
        else:
            adj = flat(k.ADJ[:, :, :])
            most = adj[:, 0:(NT - 1) * (NP + P)].rearrange("p (t q) -> p t q", q=NP + P)[:, :, 0:P]
            pool.tensor_tensor(most, most, k.loops_h[:, :].unsqueeze(1).to_broadcast([P, NT - 1, P]),
                               ALU.subtract).then_inc(s.loops_gone, 1)
            end = adj[:, (NT - 1) * (NP + P):NT * NP]
            pool.tensor_tensor(end, end, k.loops_h[:, :], ALU.subtract).then_inc(s.loops_gone, 1)
            pool.wait_ge(s.back, 16)
            pool.wait_ge(s.vectors, 3 * 16)
            pool.tensor_tensor(R[:, :, :], R[:, :, :], down(beta[:, :]), ALU.add).then_inc(s.shifted, 1)
            for g in range(NG):
                pool.wait_ge(s.third, g + 1)
                pool.tensor_tensor(tiles(k.X, g), tiles(k.X, g), tiles(k.H, g), ALU.add).then_inc(s.fourth, 1)

    @block.vector
    def _(dve):
        chain = Chain(dve, s.chain)
        dve.wait_ge(s.vectors, 3 * 16)
        dve.wait_ge(s.sums_ready, 1)
        chain(nc.vector.scalar_tensor_tensor(out=mean[:, :], in0=sums, scalar=1.0 / N, in1=mscale[:, :],
                                             op0=ALU.mult, op1=ALU.mult))
        for g in range(NG):
            dve.tensor_tensor(tiles(k.H, g), tiles(k.H, g), down(mean[:, :], G), ALU.subtract).then_inc(s.centred_h, 1)
        dve.wait_ge(s.squares_ready, 1)
        dve.tensor_scalar(scale[:, :], squares, 1.0 / N, GN_EPS, ALU.mult, ALU.add).then_inc(s.var_h, 1)
        dve.wait_ge(s.dev_h, 1)
        chain(dve.reciprocal(scale[:, :], dev[:, :]))
        chain(dve.tensor_tensor(scale[:, :], scale[:, :], weight[:, :], ALU.mult))
        if last:
            dve.wait_ge(s.shifted, 1)

        def step(n, g):
            H = tiles(k.H, g)
            if n == 0:
                dve.tensor_tensor(H, H, down(scale[:, :], G), ALU.mult).then_inc(s.first, 1)
            elif n == 1 and last:
                dve.wait_ge(s.first, g + 1)
                dve.tensor_tensor(H, H, tiles(R, g), ALU.add).then_inc(s.second, 1)
            elif n == 2:
                dve.wait_ge(s.second, g + 1)
                nc.vector.scalar_tensor_tensor(out=H, in0=H, scalar=0.01, in1=H, op0=ALU.mult, op1=ALU.max).then_inc(s.third, 1)
            elif n == 4:
                dve.wait_ge(s.fourth, g + 1)
                dve.tensor_reduce(group(k.s1, g), tiles(k.X, g), axis=AX, op=ALU.add).then_inc(s.fifth, 1)

        steps = 5 if last else 3
        for q in range(NG + steps - 1):
            for n in range(steps):
                if 0 <= q - n < NG:
                    step(n, q - n)
        if last:
            dve.wait_ge(s.fifth, NG)
            chain(dve.tensor_scalar(k.s1[:, :], k.s1[:, :], 1.0 / C, None, ALU.mult))
            for g in range(NG):
                dve.tensor_tensor(tiles(k.H, g), tiles(k.X, g), across(group(k.s1, g)), ALU.subtract).then_inc(s.centred, 1)
                if g >= 1:
                    dve_square_sum(k, dve, g - 1, s.squared, s.read)
            dve_square_sum(k, dve, NG - 1, s.squared, s.read)
            dve_normalise(nc, k, dve, chain, s.read, s.variance, s.deviation, s.normal, k.dis[:, :], s.high, s.y_ready)

    @block.scalar
    def _(act):
        for g in range(NG):
            act.wait_ge(s.centred_h, g + 1)
            nc.scalar.activation(tiles(k.T, g), tiles(k.H, g), ACT.Square).then_inc(s.squared_h, 1)
        act.wait_ge(s.var_h, 1)
        nc.scalar.activation(dev[:, :], scale[:, :], ACT.Sqrt).then_inc(s.dev_h, 1)
        if last:
            for g in range(NG):
                act_square(nc, k, act, g, s.centred, s.squared, s.read)
            act_deviation(nc, k, act, s.variance, s.deviation)
            for g in range(NG):
                act.wait_ge(s.normal, g + 1)
                act_high(nc, k, g, s.high)

    @block.tensor
    def _(pe):
        assert REST == 1
        nc.tensor.matmul(sums, k.ones[:, :], k.column_sums, start=True, stop=False)
        nc.tensor.matmul(sums, k.ones[0:LAST, :], k.H[0:LAST, NT - 1, :], start=False, stop=True).then_inc(s.sums_ready, 1)
        for g in range(NG):
            last_sum = pe_column_sums(nc, k, pe, s.squared_h, k.T, squares, g)
        last_sum.then_inc(s.squares_ready, 1)


BATCH = 5
NBATCH = NT // BATCH
BEHIND = 2


def sum_over_sources(nc, k, d, c, block):
    s = semaphores(nc, k, "l3", "chain turned copied_v copied_a used emptied final stored")
    back = flat(k.R[:, :, :])[:, 0:NBATCH * BATCH * P // 2].bitcast(F16).rearrange("p (m q) -> p m q", m=NBATCH)
    bank = [k.ps[:, b, 0:BATCH * P // 2].bitcast(F16) for b in range(NBATCH)]
    share = {0: (NBATCH + 1) // 2, 1: NBATCH // 2}

    def copied(eng, j, m):
        eng.wait_ge(s.copied_v if m % 2 else s.copied_a, j * share[m % 2] + (m // 2 + 1))

    def may_copy(eng, j, m):
        eng.wait_ge(s.turned, j * NBATCH + (m + 1))
        if j:
            eng.wait_ge(s.used, j * NBATCH + (m + 1 - NBATCH))

    @block.vector
    def _(dve):
        chain = Chain(dve, s.chain)
        def copies(j):
            for m in range(1, NBATCH, 2):
                may_copy(dve, j, m)
                dve.tensor_copy(back[:, m, :], bank[m]).then_inc(s.copied_v, 1)

        def collect(j):
            dve.wait_ge(s.used, (j + 1) * NBATCH)
            add_parts(nc, k, tiles(k.H, j, 1), 5 + j % 3).then_inc(s.emptied, 1)
            if j % G == G - 1:
                g = j // G
                dve.wait_ge(s.emptied, j + 1)
                chain(unscaled(nc, k, k.dis, g))
                dve.tensor_tensor(tiles(k.X, g), tiles(k.X, g), tiles(k.H, g), ALU.add).then_inc(s.final, 1)

        copies(0)
        for j in range(NT):
            if j + 1 < NT:
                copies(j + 1)
            collect(j)

    @block.scalar
    def _(act):
        for j in range(NT):
            for m in range(0, NBATCH, 2):
                may_copy(act, j, m)
                nc.scalar.activation(back[:, m, :], bank[m], ACT.Copy).then_inc(s.copied_a, 1)

    @block.tensor
    def _(pe):
        def turn(j, m):
            if j:
                copied(pe, j - 1, m)
            for i in range(BATCH):
                last = nc.tensor.transpose(bank[m][:, i * P:(i + 1) * P],
                                           k.ADJ[:, j, (m * BATCH + i) * P:(m * BATCH + i + 1) * P], k.ident_h[:, :])
            last.then_inc(s.turned, 1)

        def use(j, m):
            copied(pe, j, m)
            if j == 0:
                pe.wait_ge(k.y_ready, m + 1)
            if m == 0 and j >= 3:
                pe.wait_ge(s.emptied, j - 2)
            for i in range(BATCH):
                last = nc.tensor.matmul(k.ps[:, 5 + j % 3, 0:ONE], back[:, m, i * P:(i + 1) * P], k.Y[:, m * BATCH + i, 0:ONE],
                                        start=m == 0 and i == 0, stop=m == NBATCH - 1 and i == BATCH - 1)
            last.then_inc(s.used, 1)

        pe.wait_ge(k.loops_gone, 2)
        for q in range(NT * NBATCH + BEHIND):
            if q < NT * NBATCH:
                turn(*divmod(q, NBATCH))
            if q >= BEHIND:
                use(*divmod(q - BEHIND, NBATCH))

    @block.sync
    def _(sp):
        for g in range(NG):
            sp.wait_ge(s.final, g + 1)
            if g < NG - 1:
                sp.dma_start(d.out[g * G * P:(g + 1) * G * P, :].rearrange("(t p) f -> p t f", p=P),
                             tiles(k.X, g)).then_inc(s.stored, 16)
        sp.dma_start(d.out[(NG - 1) * G * P:(NT - 1) * P, :].rearrange("(t p) f -> p t f", p=P),
                     k.X[:, (NG - 1) * G:NT - 1, :]).then_inc(s.stored, 16)
        sp.dma_start(d.out[(NT - 1) * P:N, :], k.X[0:LAST, NT - 1, :]).then_inc(s.stored, 16)
        sp.wait_ge(s.stored, (NG + 1) * 16)


class OnChip:
    pass


def network(nc, d):
    with ExitStack() as c:
        def sb(name, shape, dt):
            return c.enter_context(nc.sbuf_tensor(name, shape, dt))

        k = OnChip()
        k.held = []
        k.ADJ = sb("adjacency", [P, NT, NP], F16)
        k.X = sb("x_sb", [P, NT, C], F32)
        k.ident, k.ident_h, k.loops_h = sb("ident", [P, P], F32), sb("ident_h", [P, P], F16), sb("loops_h", [P, P], F16)
        k.ones, k.ones_h = sb("ones", [P, P], F32), sb("ones_h", [P, 2], F16)
        k.out_deg, k.mean0, k.var0 = (sb(n, [P, NT], F32) for n in ("out_deg", "mean0", "var0"))
        with ExitStack() as c2:
            k.start_i = c2.enter_context(nc.sbuf_tensor("start_i", [1, NW], I32))
            locate_and_load(nc, k, d)
            build_adjacency(nc, k, d)
        k.H = sb("h_sb", [P, NT, C], F32)
        y32 = sb("y_sb", [P, NT * (C + 2) + 2 * CW + C], F32)[:, :]
        k.Y = y32[:, 0:NT * YC // 2].bitcast(F16).rearrange("p (t f) -> p t f", f=YC)
        k.T = y32[:, 0:NT * C].rearrange("p (t f) -> p t f", f=C)
        k.Hg = y32[:, 0:NT * (C + 2)].rearrange("p (t f) -> p t f", f=C + 2)
        k.spare = y32[:, NT * (C + 2):]
        k.T2 = y32[:, NT * YC // 2:NT * YC // 2 + 2 * G * C].rearrange("p (a t f) -> p a t f", a=2, f=C)
        k.clipped, k.roots = sb("clipped", [P, 2, NT], F32), sb("roots", [P, 2, NT], F32)
        k.out_norm = k.roots[:, 0, :]
        k.s1, k.s2, k.s3, k.in_norm, k.in_deg, k.inv_deg, k.dis, k.a_s, k.a_s5, k.a_unit, k.a_d = (
            sb(n, [P, NT], F32) for n in "s1 s2 s3 in_norm in_deg inv_deg dis a_s a_s5 a_unit a_d".split())
        k.column_sums = k.spare[:, 2 * CW:2 * CW + C]
        k.unscale = sb("unscale", [P, 2], F32)
        k.wide = sb("wide", [1, 1], I32)
        k.ps = c.enter_context(nc.psum_tensor("banks", [P, 8, 512], F32))
        with phases(nc) as (c, block):
            convolutions(nc, k, d, c, block)
            sage(nc, k, d, c, block)
            prepare_attention(nc, k, d, c, block, "prep1", d.W1, d.att_src1, d.att_dst1, True)
        attend(nc, k, d, "gat1", d.gat_b1)
        clear_semaphores(nc, k)
        with phases(nc) as (c, block):
            graph_norm(nc, k, d, c, block, "norm1", False)
            prepare_attention(nc, k, d, c, block, "prep2", d.W2, d.att_src2, d.att_dst2, False)
        attend(nc, k, d, "gat2", d.gat_b2)
        with phases(nc) as (c, block):
            graph_norm(nc, k, d, c, block, "norm2", True)
            sum_over_sources(nc, k, d, c, block)


INPUTS = {
    "x": "x", "src": "src", "dst": "dst",
    "L0_gnn_bias1": "bias1", "L0_gnn_bias2": "bias2", "L0_gnn_gamma": "gamma", "L0_gnn_beta": "beta",
    "L1_gnn_W_self1": "W_self1", "L1_gnn_W_neigh1": "W_neigh1", "L1_gnn_b1": "b1",
    "L1_gnn_W_self2": "W_self2", "L1_gnn_W_neigh2": "W_neigh2", "L1_gnn_b2": "b2",
    "L2_gnn_W1": "W1", "L2_gnn_att_src1": "att_src1", "L2_gnn_att_dst1": "att_dst1", "L2_gnn_b1": "gat_b1",
    "L2_gnn_W2": "W2", "L2_gnn_att_src2": "att_src2", "L2_gnn_att_dst2": "att_dst2", "L2_gnn_b2": "gat_b2",
    "L2_gnn_gn_weight": "gn_weight", "L2_gnn_gn_bias": "gn_bias", "L2_gnn_gn_mean_scale": "gn_mean_scale",
}


def program(nc, shapes):
    arrays = {short: nc.dram_tensor(f"in_{name}", shapes[name][0], shapes[name][1], kind="ExternalInput").ap()
              for name, short in INPUTS.items()}
    arrays["keys"] = nc.dram_tensor("edge_keys", [E], I32).ap()
    arrays["residual"] = nc.dram_tensor("residual", [P, NT, C], F32).ap()
    arrays["out"] = nc.dram_tensor("out_x", [N, C], F32, kind="ExternalOutput").ap()
    d = namedtuple("Dram", list(arrays))(*arrays.values())
    network(nc, d)


def kernel(**inputs):
    import numpy as np
    import concourse.bacc as bacc
    from concourse.bass_utils import run_bass_kernel_spmd

    nc = bacc.Bacc("TRN2", target_bir_lowering=False, num_devices=1)
    arrays = {f"in_{name}": np.ascontiguousarray(inputs[name]) for name in INPUTS}
    program(nc, {name: (arrays[f"in_{name}"].shape, mybir.dt.from_np(arrays[f"in_{name}"].dtype)) for name in INPUTS})
    r = run_bass_kernel_spmd(nc, [arrays], core_ids=[0])
    return r.results[0]["out_x"]
```
